# Optimizing a Trainium2 kernel written in Bass

```python
import numpy as np
import jax
import jax.numpy as jnp

def _softmax(x, axis=-1):
    return jax.nn.softmax(x, axis=axis)

def _gelu(x):
    return jax.nn.gelu(x, approximate=True)

def _silu(x):
    return jax.nn.silu(x)

def _sigmoid(x):
    return jax.nn.sigmoid(x)

def _layernorm(x, axis=-1, eps=1e-05):
    m = jnp.mean(x, axis=axis, keepdims=True)
    v = jnp.var(x, axis=axis, keepdims=True)
    return (x - m) / jnp.sqrt(v + eps)

def _scatter_add(tgt, idx, src, axis=0):
    return tgt.at[idx].add(src)

def _segment_sum(src, seg, n):
    return jax.ops.segment_sum(src, seg, n)
kernel_name = 'mk_adj_resnorm_d1_adj_r2_369131'

def setup_inputs(seed: int=0):
    np.random.seed(seed)
    _w = jnp.asarray

    def _rec_inputs():
        import jax
        import jax.numpy as jnp
        _gk = jax.random.key(seed)
        x = -9.806e-05 + 1 * jax.random.normal(jax.random.fold_in(_gk, 1), (8192, 128), jnp.float32)
        _a = jax.random.bernoulli(jax.random.fold_in(_gk, 2), 0.00195312, (8192, 8192))
        _a = jnp.logical_or(_a, jnp.swapaxes(_a, -1, -2))
        _a = jnp.logical_or(_a, jnp.eye(8192, dtype=bool))
        _af = _a.astype(jnp.float32)
        _af = _af * jax.random.uniform(jax.random.fold_in(_gk, 3), (8192, 8192), jnp.float32, 0.05, 1)
        adj = _af
        return (x, adj)
    x, adj = _rec_inputs()

    def _L0_gnn_setup():
        import jax, jax.numpy as jnp
        import numpy as np

        def _lap_mul(A, x):
            d = 1.0 / jnp.sqrt(jnp.sum(A, axis=-1))
            return d[:, None] * (A @ (d[:, None] * x))
        key = jax.random.key(seed)
        k1, k2, k3, k4, k5, k6 = jax.random.split(key, 6)
        N, D_IN, D_OUT = (2048, 128, 128)
        x = jax.random.normal(k1, (N, D_IN), dtype=jnp.float32)
        A = jax.random.uniform(k2, (N, N), dtype=jnp.float32)
        s1 = 1.0 / np.sqrt(D_IN)
        W1 = jax.random.uniform(k3, (D_IN, D_OUT), minval=-s1, maxval=s1, dtype=jnp.float32)
        b1 = jax.random.uniform(k4, (D_OUT,), minval=-s1, maxval=s1, dtype=jnp.float32)
        W2 = jax.random.uniform(k5, (D_IN, D_OUT), minval=-s1, maxval=s1, dtype=jnp.float32)
        b2 = jax.random.uniform(k6, (D_OUT,), minval=-s1, maxval=s1, dtype=jnp.float32)
        return {'x': x, 'A': A, 'W1': W1, 'b1': b1, 'W2': W2, 'b2': b2, 'sigma': 1, 'k': 4}
    _L0_gnn_all = _L0_gnn_setup()
    _L0_gnn_in = {k: v for k, v in _L0_gnn_all.items() if k in ('W1', 'b1', 'W2', 'b2')}
    del _L0_gnn_all
    return {'x': x, 'adj': adj, 'L0_gnn_W1': _L0_gnn_in['W1'], 'L0_gnn_b1': _L0_gnn_in['b1'], 'L0_gnn_W2': _L0_gnn_in['W2'], 'L0_gnn_b2': _L0_gnn_in['b2']}

def reference(x, adj, L0_gnn_W1, L0_gnn_b1, L0_gnn_W2, L0_gnn_b2):
    import jax
    import jax.numpy as jnp

    def _L0_gnn_ref(x, A, W1, b1, W2, b2, sigma, k):
        import jax, jax.numpy as jnp
        import numpy as np

        def _lap_mul(A, x):
            d = 1.0 / jnp.sqrt(jnp.sum(A, axis=-1))
            return d[:, None] * (A @ (d[:, None] * x))
        z = _lap_mul(A, x) @ W1 + b1
        z = jax.nn.leaky_relu(z, negative_slope=0.1)
        sq = jnp.sum(z * z, axis=-1)
        d2 = sq[:, None] + sq[None, :] - 2.0 * (z @ z.T)
        d2 = jnp.maximum(d2, 0.0)
        S = jnp.sqrt(d2 + 1e-10)
        S = jnp.exp(-S / (2.0 * sigma))
        order = jnp.argsort(-S, axis=-1)
        ranks = jnp.argsort(order, axis=-1)
        S = jnp.where(ranks < k, S, 0.0)
        A2 = S + A
        out = _lap_mul(A2, x) @ W2 + b2
        return out
    x = _layernorm(x + _L0_gnn_ref(x, adj, L0_gnn_W1, L0_gnn_b1, L0_gnn_W2, L0_gnn_b2, 1, 4), axis=-1)
    return x

_drawn_inputs = setup_inputs


def setup_inputs(seed=0):
    import zlib

    import numpy as np

    out = dict(_drawn_inputs(seed))
    spreads = {}
    factors = {}
    for name, (base, spread) in spreads.items():
        noise = np.random.default_rng([zlib.crc32(name.encode()), seed]).standard_normal(out[name].shape)
        drawn = base * np.exp(spread * noise) if base else spread * noise
        out[name] = jnp.asarray(drawn.astype(out[name].dtype))
    for name, factor in factors.items():
        out[name] = (out[name] * factor).astype(out[name].dtype)
    return out
```

```python
from contextlib import ExitStack

import concourse.bass as bass
from concourse import mybir

P = 128
N = 8192
D = 128
NB = N // P
SB = 1024
NS = N // SB
BS = SB // P
CH = 512
HB = BS // 2
RING = 3
TOPK = 4
EPS_D2 = 1e-10
EPS_LN = 1e-5

ALU = mybir.AluOpType
ACT = mybir.ActivationFunctionType
AX = mybir.AxisListType
F32 = mybir.dt.float32
BF16 = mybir.dt.bfloat16
U32 = mybir.dt.uint32

TILES_A = NS * NS
TILES_B = NS * (NS - 1) // 2
C0 = TILES_A + TILES_B
QB = NS * (NS + 1) // 2
QC = QB + TILES_B


def gnn_kernel(nc, at, xt, x, w1, b1, w2, b2, out, q_dram):
    with ExitStack() as ctx:
        def sb(name, shape, dt=F32):
            return ctx.enter_context(nc.sbuf_tensor(name, shape, dt))

        def sem(name):
            return ctx.enter_context(nc.semaphore(name))

        ring = sb("ring", [P, RING, BS, SB])
        Y = sb("Y", [P, NB, D])
        U = sb("U", [P, N])
        sqp = sb("sqp", [P, N], BF16)
        ystage = sb("ystage", [P, 2, HB, D])
        ptmp = sb("ptmp", [P, 2, CH])
        part = sb("part", [P, SB])
        rsum = sb("rsum", [P, SB])
        diag = sb("diag", [P, BS, P])
        ztmp = sb("ztmp", [P, CH])
        xts = sb("xts", [P, 2, CH])
        ident = sb("ident", [P, P])
        ones = sb("ones", [P, P])
        negsel = sb("negsel", [P, P], BF16)
        w2s = sb("w2s", [P, D])
        b1s = sb("b1s", [P, 1])
        b2b = sb("b2b", [P, 1, D])
        rn = sb("rn", [P, NB])
        dn = sb("dn", [P, NB])
        sqn = sb("sqn", [P, NB])
        d2n = sb("d2n", [P, NB])
        mhalf = sb("mhalf", [P, NB])
        top8 = sb("top8", [P, 2, 8])
        idx8 = sb("idx8", [P, 2, 8], U32)
        gidx = sb("gidx", [P, 2, TOPK], U32)
        stat = sb("stat", [P, 4, BS])

        w1s = diag[:, 0, :]
        b2r = diag[0:1, 1, :]
        zsq, resid = part, rsum
        rows = [ring[:, q, :, :].rearrange("p b i -> p (b i)") for q in range(2)]
        zst = rsum[:, 0:2 * P].rearrange("p (q i) -> p q i", q=2)
        topv = part[:, 0:NB * TOPK].rearrange("p (b k) -> p b k", k=TOPK)
        S = part[:, NB * TOPK:2 * NB * TOPK].rearrange("p (b k) -> p b k", k=TOPK)
        topi = part[:, 2 * NB * TOPK:3 * NB * TOPK].bitcast(U32).rearrange("p (b k) -> p b k", k=TOPK)
        acc, gsum, xin, obuf, osq, gath = (U[:, t * SB:(t + 1) * SB] for t in range(6))
        gsum, xin, obuf, osq = (v.rearrange("p (b d) -> p b d", b=BS) for v in (gsum, xin, obuf, osq))
        G = gath.rearrange("p (q k d) -> p q k d", q=2, k=TOPK)

        ps = ctx.enter_context(nc.psum_tensor("ps", [P, 8, CH], F32))
        PROD, BC, SQ, SMALL = 0, 2, 4, 6

        half_sem = [sem(f"half_sem{s}") for s in range(2 * RING)]
        half_loaded = sem("half_loaded")
        consts_in = sem("consts_in")
        const_step = sem("const_step")
        neg_step = sem("neg_step")
        xt_sem = [sem(f"xt_sem{q}") for q in range(2)]
        proj_done = sem("proj_done")
        proj_used = sem("proj_used")
        staged = [sem(f"staged{h}") for h in range(2)]
        w0_used = sem("w0_used")
        chunk_done = [sem(f"chunk_done{c}") for c in range(2)]
        evicted = [sem(f"evicted{c}") for c in range(2)]
        added = [sem(f"added{c}") for c in range(2)]
        part_done = sem("part_done")
        row_step = sem("row_step")
        rnat_done = sem("rnat_done")
        rn_copied = sem("rn_copied")
        d_ready = sem("d_ready")
        y_ready = sem("y_ready")
        u_done = sem("u_done")
        diag_ready = sem("diag_ready")
        bc_done = sem("bc_done")
        z_step = sem("z_step")
        zsq_ready = sem("zsq_ready")
        sq_done = sem("sq_done")
        sqn_copied = sem("sqn_copied")
        split_step = sem("split_step")
        z_staged = sem("z_staged")
        scores_done = sem("scores_done")
        banks_free = sem("banks_free")
        max_done = sem("max_done")
        row_free = sem("row_free")
        top_kept = sem("top_kept")
        dist_step = sem("dist_step")
        root_done = sem("root_done")
        s_ready = sem("s_ready")
        deg_step = sem("deg_step")
        d2_ready = sem("d2_ready")
        q_ready = sem("q_ready")
        q_stored = sem("q_stored")
        gidx_ready = sem("gidx_ready")
        g_sem = [sem(f"g_sem{q}") for q in range(2)]
        g_step = sem("g_step")
        turned = sem("turned")
        x_loaded = sem("x_loaded")
        ln_step = sem("ln_step")
        rstd_ready = sem("rstd_ready")
        out_stored = sem("out_stored")
        passed = sem("passed")

        Z_OPS, SPLIT_OPS, LN_OPS = 6, 5, 11

        def products_before(n):
            if n >= TILES_A:
                return QB + n - TILES_A
            i, r = divmod(n, NS)
            return i * (i + 1) // 2 + max(0, r - (NS - 1 - i))

        def over(column, n):
            return column.rearrange("p (b a) -> p b a", a=1).to_broadcast([P, BS, n])

        def plain(engine):
            engine.sem_inc(passed, 1)

        x_rows = x.rearrange("(i b p) d -> i p b d", b=BS, p=P)
        out_rows = out.rearrange("(i b p) d -> i p b d", b=BS, p=P)

        block = ctx.enter_context(nc.Block())

        @block.sync
        def _(sp):
            for dst, src in ((w1s, w1), (w2s[:, :], w2), (b1s[:, :], b1), (b2r, b2)):
                sp.dma_start(dst, src).then_inc(consts_in, 16)

            def pass_on(slot, h, turn):
                sp.wait_ge(half_sem[2 * slot + h], turn * 16 + 16)
                sp.sem_inc(half_loaded, 1)

            tiles = [(i, r) for i in range(NS) for r in range(NS)]
            tiles += [(NS - 1 - m, r) for m in range(1, NS) for r in range(m)]
            for n, (i, r) in enumerate(tiles):
                slot = n % RING
                if n >= RING:
                    sp.wait_ge(part_done, min(n - RING + 1, TILES_A))
                    if products_before(n - RING + 1):
                        sp.wait_ge(chunk_done[1], products_before(n - RING + 1))
                for h in range(2):
                    sp.dma_start(ring[:, slot, h * HB:(h + 1) * HB, :],
                                 at[i * NS + r, :, h * HB:(h + 1) * HB, :]).then_inc(half_sem[2 * slot + h], 16)
                    if n:
                        pass_on((n - 1) % RING, h, (n - 1) // RING)
            for h in range(2):
                pass_on((C0 - 1) % RING, h, (C0 - 1) // RING)

            def tile_c(c, t, g):
                slot, before = (C0 + t) % RING, (C0 + t - 1) % RING
                sp.wait_ge(chunk_done[1], c + (QC - RING + 1))
                for h in range(2):
                    sp.dma_start(ring[:, slot, h * HB:(h + 1) * HB, :],
                                 at[c, :, h * HB:(h + 1) * HB, :]).then_inc(half_sem[2 * slot + h], 16)
                    if not (isinstance(c, int) and c == 0):
                        pass_on(before, h, g + (C0 + t - 1) // RING)

            tile_c(0, 0, 0)
            sp.wait_ge(row_free, 2 + NB)
            tile_c(1, 1, 0)
            tile_c(2, 2, 0)
            with sp.Fori(1, NS * NS // RING) as g:
                for t in range(RING):
                    tile_c(g * RING + t, t, g)
            tile_c(NS * NS - 1, 0, NS * NS // RING)
            for h in range(2):
                pass_on((C0 + NS * NS - 1) % RING, h, (C0 + NS * NS - 1) // RING)

        @block.tensor
        def _(pe):
            def project(s0, w):
                with pe.Fori(0, NB // (2 * HB)) as g:
                    for q in range(2):
                        pe.wait_ge(xt_sem[q], g * 16 + (s0 // 2 * 16 + 16))
                        pe.wait_ge(proj_used, g * 2 + (s0 + q))
                        for b in range(HB):
                            mm = pe.matmul(ps[:, BC + q, b * D:(b + 1) * D], xts[:, q, b * P:(b + 1) * P],
                                           w, start=True, stop=True)
                        mm.then_inc(proj_done, 1)

            def product(q, n):
                for c in range(2):
                    if not (isinstance(q, int) and q == 0):
                        pe.wait_ge(evicted[c], q)
                    for b in range(BS):
                        if c == 0 and b % HB == 0:
                            pe.wait_ge(half_loaded, n * 2 + (1 + b // HB))
                            pe.wait_ge(staged[b // HB], q + 1)
                        mm = pe.matmul(ps[:, PROD + c, :], ystage[:, b // HB, b % HB, :],
                                       ring[:, n % RING, b, c * CH:(c + 1) * CH],
                                       start=(b == 0), stop=(b == BS - 1))
                        if c == 1 and b == HB - 1:
                            mm.then_inc(w0_used, 1)
                    mm.then_inc(chunk_done[c], 1)

            def spread_d(f):
                pe.wait_ge(diag_ready, f + 1)
                if f:
                    pe.wait_ge(z_step, Z_OPS * f)
                for c in range(2):
                    mm = pe.matmul(ps[:, BC + c, :], ones[:, :],
                                   diag[:, c * HB:(c + 1) * HB, :].rearrange("p b i -> p (b i)"),
                                   start=True, stop=True)
                mm.then_inc(bc_done, 1)

            def squares(f):
                pe.wait_ge(zsq_ready, f + 1)
                if f:
                    pe.wait_ge(split_step, SPLIT_OPS * f)
                    pe.wait_ge(sqn_copied, f)
                for c in range(2):
                    pe.matmul(ps[:, SQ + c, :], ones[:, :], zsq[:, c * CH:(c + 1) * CH], start=True, stop=True)
                for b in range(BS):
                    mm = pe.matmul(ps[:, SMALL, b:b + 1], zsq[:, b * P:(b + 1) * P], ones[:, 0:1],
                                   start=True, stop=True)
                mm.then_inc(sq_done, 1)

            pe.wait_ge(const_step, 2)
            pe.wait_ge(consts_in, 64)
            pe.matmul(ps[:, SMALL, 0:D], ones[0:1, :], b2r, start=True, stop=True).then_inc(proj_done, 1)
            project(0, w1s)
            pe.wait_ge(proj_used, 1)
            for i in range(NS):
                q0 = i * (i + 1) // 2
                if i:
                    with pe.Fori(0, i) as k:
                        product(k + q0, k + (NS * i + NS - 1 - i))
                pe.wait_ge(row_step, NS * (i + 1))
                if i:
                    pe.wait_ge(rn_copied, i)
                for b in range(BS):
                    mm = pe.matmul(ps[:, SMALL, b:b + 1], rsum[:, b * P:(b + 1) * P], ones[:, 0:1],
                                   start=True, stop=True)
                mm.then_inc(rnat_done, 1)
                product(q0 + i, NS * i + NS - 1)
            pe.wait_ge(proj_used, 1 + NB // HB)
            spread_d(0)
            pe.wait_ge(rn_copied, NS)
            for m in range(1, NS):
                q0 = QB + m * (m - 1) // 2
                with pe.Fori(0, m) as k:
                    product(k + q0, k + (q0 - QB + TILES_A))
                squares(m - 1)
                spread_d(m)
            pe.wait_ge(z_step, Z_OPS * NS - 1)
            project(NB // HB, w2s[:, :])
            squares(NS - 1)

            pe.wait_ge(split_step, SPLIT_OPS * NS)
            with pe.Fori(0, NB // 2) as g:
                for q in range(2):
                    pe.wait_ge(z_staged, g * 2 + (q + 1))
                    for cc in range(NS):
                        pair = 2 * (cc % 2)
                        pe.wait_ge(banks_free, g * (2 * NS) + (NS * q + cc + 1))
                        for c in range(2):
                            cols = slice((2 * cc + c) * CH, (2 * cc + c + 1) * CH)
                            pe.matmul(ps[:, pair + c, :], zst[:, q, :], U[:, cols], start=True, stop=False)
                            mm = pe.matmul(ps[:, pair + c, :], negsel[:, :], sqp[:, cols], start=False, stop=True)
                        mm.then_inc(scores_done, 1)

            pe.wait_ge(banks_free, 2 + NS * NB)
            with pe.Fori(0, NS) as i:
                with pe.Fori(0, NS) as r:
                    product(i * NS + r + QC, i * NS + r + C0)
                for c in range(2):
                    pe.wait_ge(added[c], i * NS + (QC + NS))
                pe.wait_ge(ln_step, i * LN_OPS)
                for b in range(BS):
                    mm = pe.transpose(ps[:, BC + b // HB, (b % HB) * P:(b % HB + 1) * P],
                                      acc[:, b * P:(b + 1) * P], ident[:, :])
                mm.then_inc(turned, 1)

        @block.scalar
        def _(act):
            def load_xt(s, q):
                act.dma_start(xts[:, q, :], xt[:, bass.ds(s * CH, CH)]).then_inc(xt_sem[q], 16)

            def keep_projection(s, q):
                act.wait_ge(proj_done, s + 2)
                act.activation(Y[:, bass.ds((s % (NB // HB)) * HB, HB), :].rearrange("p b d -> p (b d)"),
                               ps[:, BC + q, :], ACT.Copy).then_inc(proj_used, 1)

            def stage(q, j, h):
                if not (isinstance(q, int) and q == 0):
                    act.wait_ge(chunk_done[1] if h else w0_used, q)
                act.activation(ystage[:, h, :, :], Y[:, bass.ds(j * BS + h * HB, HB), :],
                               ACT.Copy).then_inc(staged[h], 1)

            def evict(q, c):
                act.wait_ge(chunk_done[c], q + 1)
                if not (isinstance(q, int) and q == 0):
                    act.wait_ge(added[c], q)
                act.activation(ptmp[:, c, :], ps[:, PROD + c, :], ACT.Copy).then_inc(evicted[c], 1)

            def step(q, j):
                for h in range(2):
                    evict(q - 1, h)
                    stage(q, j, h)

            def first(q, j):
                for h in range(2):
                    stage(q, j, h)

            def flush(q):
                for c in range(2):
                    evict(q, c)

            load_xt(0, 0)
            load_xt(1, 1)
            act.wait_ge(proj_done, 1)
            act.activation(b2b[:, 0, :], ps[:, SMALL, 0:D], ACT.Copy).then_inc(proj_used, 1)
            with act.Fori(0, NB // HB // 2) as g:
                for q in range(2):
                    keep_projection(g * 2 + q, q)
                    load_xt((g * 2 + (q + 2)) % (NB // HB), q)

            for i in range(NS):
                q0 = i * (i + 1) // 2
                if i:
                    first(q0, 0)
                if i > 1:
                    with act.Fori(1, i) as k:
                        step(k + q0, k)
                act.wait_ge(rnat_done, i + 1)
                act.activation(rn[:, i * BS:(i + 1) * BS], ps[:, SMALL, 0:BS], ACT.Copy).then_inc(rn_copied, 1)
                if i:
                    flush(q0 + i - 1)
                act.wait_ge(y_ready, i + 1)
                first(q0 + i, i)
                flush(q0 + i)

            def square(f):
                act.wait_ge(z_step, Z_OPS * (f + 1))
                if f:
                    act.wait_ge(sq_done, f)
                act.activation(zsq[:, :], U[:, (NS - 1 - f) * SB:(NS - f) * SB],
                               ACT.Square).then_inc(zsq_ready, 1)

            def keep_squares(f):
                act.wait_ge(sq_done, f + 1)
                act.activation(sqn[:, (NS - 1 - f) * BS:(NS - f) * BS], ps[:, SMALL, 0:BS],
                               ACT.Copy).then_inc(sqn_copied, 1)

            act.wait_ge(row_step, NS * NS)
            for m in range(1, NS):
                q0 = QB + m * (m - 1) // 2
                first(q0, NS - m)
                square(m - 1)
                if m > 1:
                    with act.Fori(1, m) as k:
                        step(k + q0, k + (NS - m))
                flush(q0 + m - 1)
                keep_squares(m - 1)

            for h in range(2):
                act.wait_ge(staged[h], QC)
            square(NS - 1)
            with act.Fori(0, NB // HB // 2 - 1) as g:
                for q in range(2):
                    keep_projection(g * 2 + (q + NB // HB), q)
                    load_xt(g * 2 + (q + 2), q)
            for q in range(2):
                keep_projection(2 * NB // HB - 2 + q, q)
            keep_squares(NS - 1)

            act.wait_ge(split_step, SPLIT_OPS * NS)
            act.wait_ge(proj_used, 1 + 2 * NB // HB)
            for c in range(2):
                act.wait_ge(evicted[c], QC)
            act.sem_inc(banks_free, 2)
            with act.Fori(0, NB // 2) as g:
                for q in range(2):
                    act.wait_ge(row_free, g * 2 + (q + 1))
                    for cc in range(NS):
                        act.wait_ge(scores_done, g * (2 * NS) + (NS * q + cc + 1))
                        act.activation(rows[q][:, cc * SB:(cc + 1) * SB],
                                       ps[:, 2 * (cc % 2):2 * (cc % 2) + 2, :].rearrange("p c i -> p (c i)"),
                                       ACT.Copy).then_inc(banks_free, 1)

            act.wait_ge(dist_step, 2)
            act.activation(S, topv, ACT.Sqrt).then_inc(root_done, 1)
            act.wait_ge(root_done, 1)
            act.activation(S, S, ACT.Exp, scale=-0.5).then_inc(s_ready, 1)

            for j in range(NS):
                act.wait_ge(q_ready, j + 1)
                act.dma_start(q_dram[j * SB:(j + 1) * SB, :].rearrange("(b p) d -> p b d", p=P),
                              Y[:, j * BS:(j + 1) * BS, :]).then_inc(q_stored, 16)

            with act.Fori(0, NS) as i:
                first(i * NS + QC, (i + 1) % NS)
                with act.Fori(1, NS) as r:
                    step(i * NS + r + QC, (i + 1 + r) % NS)
                flush(i * NS + (QC + NS - 1))
            act.wait_ge(q_stored, 16 * NS)

        @block.vector
        def _(dve):
            with dve.Fori(0, NS) as i:
                for first in (True, False):
                    def sum_tile(n):
                        dve.wait_ge(half_loaded, n * 2 + 2)
                        dve.wait_ge(row_step, n)
                        dve.tensor_reduce(part[:, :], ring[:, n % RING, :, :].rearrange("p b i -> p i b"),
                                          AX.X, ALU.add).then_inc(part_done, 1)
                        dve.wait_ge(part_done, n + 1)
                    if first:
                        sum_tile(i * NS)
                        dve.wait_ge(rnat_done, i)
                        dve.tensor_copy(rsum[:, :], part[:, :]).then_inc(row_step, 1)
                    else:
                        with dve.Fori(1, NS) as r:
                            sum_tile(i * NS + r)
                            dve.tensor_tensor(rsum[:, :], rsum[:, :], part[:, :], ALU.add).then_inc(row_step, 1)

            dve.wait_ge(rnat_done, NS)
            with dve.Fori(0, NS) as f:
                sup = (f * (NS - 1) + (NS - 1)) % NS
                dve.wait_ge(bc_done, f + 1)
                dve.wait_ge(u_done, f + 1)
                for c in range(2):
                    u = U[:, bass.ds(sup * SB + c * CH, CH)]
                    dve.wait_ge(z_step, f * Z_OPS + 3 * c)
                    dve.tensor_tensor(ztmp[:, :], u, ps[:, BC + c, :], ALU.mult).then_inc(z_step, 1)
                    dve.wait_ge(z_step, f * Z_OPS + (3 * c + 1))
                    dve.tensor_scalar(ztmp[:, :], ztmp[:, :], b1s[:, :], None, ALU.add).then_inc(z_step, 1)
                    dve.wait_ge(z_step, f * Z_OPS + (3 * c + 2))
                    dve.scalar_tensor_tensor(out=u, in0=ztmp[:, :], scalar=0.1, in1=ztmp[:, :],
                                             op0=ALU.mult, op1=ALU.max).then_inc(z_step, 1)
                dve.wait_ge(sq_done, f + 1)
                sq = ps[:, SQ:SQ + 2, :].rearrange("p c i -> p (c i)")
                cols = bass.ds(sup * SB, SB)
                dve.tensor_copy(sqp[:, cols], sq).then_inc(split_step, 1)
                for t, p0 in enumerate((64, 96)):
                    dve.wait_ge(split_step, f * SPLIT_OPS + (2 * t + 1))
                    dve.tensor_tensor(resid[p0:P, :], sq[p0:P, :] if t == 0 else resid[p0:P, :],
                                      sqp[p0:P, cols], ALU.subtract).then_inc(split_step, 1)
                    dve.wait_ge(split_step, f * SPLIT_OPS + (2 * t + 2))
                    plain(dve)
                    dve.tensor_copy(sqp[p0:P, cols], resid[p0:P, :]).then_inc(split_step, 1)

            dve.wait_ge(sq_done, NS)
            dve.sem_inc(row_free, 2)
            with dve.Fori(0, NB // 2) as g:
                for q in range(2):
                    dve.wait_ge(banks_free, g * (2 * NS) + (NS * (q + 1) + 2))
                    dve.wait_ge(top_kept, g * 4 + 2 * q)
                    plain(dve)
                    dve.max(top8[:, q, :], rows[q]).then_inc(max_done, 1)
                    dve.wait_ge(max_done, g * 2 + (q + 1))
                    plain(dve)
                    dve.max_index(idx8[:, q, :], top8[:, q, :], rows[q]).then_inc(row_free, 1)
                    dve.tensor_copy(topv[:, bass.ds(g * 2 + q, 1), :], top8[:, q:q + 1, 0:TOPK]).then_inc(top_kept, 1)
                    dve.wait_ge(row_free, g * 2 + (q + 3))
                    dve.tensor_copy(topi[:, bass.ds(g * 2 + q, 1), :], idx8[:, q:q + 1, 0:TOPK]).then_inc(top_kept, 1)

            dve.wait_ge(top_kept, 2 * NB)
            dve.wait_ge(sqn_copied, NS)
            dve.tensor_tensor(topv, sqn.rearrange("p (b a) -> p b a", a=1).to_broadcast([P, NB, TOPK]), topv,
                              ALU.subtract).then_inc(dist_step, 1)
            dve.wait_ge(dist_step, 1)
            dve.tensor_scalar(topv, topv, 0.0, EPS_D2, ALU.max, ALU.add).then_inc(dist_step, 1)
            dve.wait_ge(s_ready, 1)
            dve.tensor_reduce(d2n[:, :], S, AX.X, ALU.add).then_inc(deg_step, 1)
            dve.wait_ge(deg_step, 1)
            dve.tensor_tensor(d2n[:, :], d2n[:, :], rn[:, :], ALU.add).then_inc(deg_step, 1)
            dve.wait_ge(d2_ready, 1)
            dve.wait_ge(proj_used, 1 + 2 * NB // HB)
            for j in range(NS):
                yj = Y[:, j * BS:(j + 1) * BS, :]
                dve.tensor_tensor(yj, yj, over(d2n[:, j * BS:(j + 1) * BS], D), ALU.mult).then_inc(q_ready, 1)

            dve.tensor_copy(gidx[:, 0, :], topi[:, 0, :]).then_inc(gidx_ready, 1)
            with dve.Fori(0, NS) as i:
                with dve.Fori(0, BS // 2) as rr:
                    for t in range(2):
                        blk = i * BS + rr * 2 + t
                        dve.wait_ge(g_step, blk * TOPK)
                        dve.tensor_copy(gidx[:, 1 - t:2 - t, :],
                                        topi[:, bass.ds((blk + 1) % NB, 1), :]).then_inc(gidx_ready, 1)
                        dve.wait_ge(g_sem[t], (i * (BS // 2) + rr + 1) * (16 * TOPK))
                        gs = gsum[:, bass.ds(rr * 2 + t, 1), :].rearrange("p a d -> p (a d)")
                        for k in range(TOPK):
                            sk = S[:, bass.ds(blk, 1), k:k + 1].rearrange("p a k -> p (a k)")
                            if k == 0:
                                dve.tensor_scalar(gs, G[:, t, k, :], sk, None, ALU.mult).then_inc(g_step, 1)
                            else:
                                dve.wait_ge(g_step, blk * TOPK + k)
                                dve.scalar_tensor_tensor(out=gs, in0=G[:, t, k, :], scalar=sk, in1=gs,
                                                         op0=ALU.mult, op1=ALU.add).then_inc(g_step, 1)
                steps = [0]

                def ln(instruction):
                    instruction.then_inc(ln_step, 1)
                    steps[0] += 1
                    dve.wait_ge(ln_step, i * LN_OPS + steps[0])

                d2i = d2n[:, bass.ds(i * BS, BS)]
                dve.wait_ge(turned, i + 1)
                dve.wait_ge(g_step, (i + 1) * (BS * TOPK))
                o = obuf.rearrange("p b d -> p (b d)")
                ln(dve.tensor_tensor(o, ps[:, BC:BC + 2, :].rearrange("p c i -> p (c i)"),
                                     gsum.rearrange("p b d -> p (b d)"), ALU.add))
                ln(dve.tensor_tensor(obuf, obuf, over(d2i, D), ALU.mult))
                dve.wait_ge(x_loaded, (i + 1) * 16)
                ln(dve.tensor_tensor(xin, xin, b2b[:, :, :].to_broadcast([P, BS, D]), ALU.add))
                ln(dve.tensor_tensor(obuf, obuf, xin, ALU.add))
                ln(dve.tensor_reduce(stat[:, 0, :], obuf, AX.X, ALU.add))
                ln(dve.tensor_scalar(stat[:, 1, :], stat[:, 0, :], 1.0 / D, None, ALU.mult))
                ln(dve.tensor_tensor(obuf, obuf, over(stat[:, 1, :], D), ALU.subtract))
                dve.wait_ge(out_stored, i * 16)
                ln(dve.tensor_tensor(osq, obuf, obuf, ALU.mult))
                ln(dve.tensor_reduce(stat[:, 2, :], osq, AX.X, ALU.add))
                ln(dve.tensor_scalar(stat[:, 3, :], stat[:, 2, :], 1.0 / D, EPS_LN, ALU.mult, ALU.add))
                dve.wait_ge(rstd_ready, i + 1)
                ln(dve.tensor_tensor(osq, obuf, over(stat[:, 3, :], D), ALU.mult))

        @block.gpsimd
        def _(pool):
            pool.memset(ident[:, :], 0.0).then_inc(const_step, 1)
            pool.memset(ones[:, :], 1.0).then_inc(const_step, 1)
            pool.memset(mhalf[:, :], -0.5).then_inc(const_step, 1)
            pool.memset(negsel[:, :], 0.0).then_inc(const_step, 1)
            pool.wait_ge(const_step, 4)
            pool.affine_select(out=ident[:, :], in_=ident[:, :], compare_op=ALU.not_equal, fill=1.0, base=0,
                               pattern=[[-1, P]], channel_multiplier=1).then_inc(neg_step, 1)
            for t, p0 in enumerate((0, 64, 96)):
                pool.wait_ge(neg_step, t + 1)
                pool.memset(negsel[p0:p0 + 1, :], -1.0).then_inc(neg_step, 1)
            pool.wait_ge(neg_step, 4)

            def add(q, row, fresh):
                for c in range(2):
                    u = U[:, row * SB + c * CH:row * SB + (c + 1) * CH]
                    pool.wait_ge(evicted[c], q + 1)
                    if fresh:
                        plain(pool)
                        pool.tensor_copy(u, ptmp[:, c, :]).then_inc(added[c], 1)
                    else:
                        pool.wait_ge(added[c], q)
                        pool.tensor_tensor(u, u, ptmp[:, c, :], ALU.add).then_inc(added[c], 1)

            def inverse_root(v, n):
                return pool.tensor_tensor(v, v, mhalf[:, 0:n], ALU.pow)

            def make_diag(f):
                if f:
                    pool.wait_ge(bc_done, f)
                j = NS - 1 - f
                pool.tensor_tensor(diag[:, :, :],
                                   ident[:, :].rearrange("p (a i) -> p a i", a=1).to_broadcast([P, BS, P]),
                                   over(dn[:, j * BS:(j + 1) * BS], P), ALU.mult).then_inc(diag_ready, 1)

            pool.wait_ge(proj_used, 1 + NB // HB)
            for i in range(NS):
                q0 = i * (i + 1) // 2
                if i > 1:
                    add(q0, i, True)
                if i > 2:
                    with pool.Fori(1, i - 1) as k:
                        add(k + q0, i, False)
                cols = slice(i * BS, (i + 1) * BS)
                pool.wait_ge(rn_copied, i + 1)
                pool.tensor_tensor(dn[:, cols], rn[:, cols], mhalf[:, 0:BS], ALU.pow).then_inc(d_ready, 1)
                pool.wait_ge(d_ready, i + 1)
                pool.tensor_tensor(Y[:, cols, :], Y[:, cols, :], over(dn[:, cols], D), ALU.mult).then_inc(y_ready, 1)
                if i:
                    add(q0 + i - 1, i, i == 1)
                add(q0 + i, i, i == 0)
            for c in range(2):
                pool.wait_ge(added[c], QB)
            pool.sem_inc(u_done, 1)
            make_diag(0)
            for m in range(1, NS):
                make_diag(m)
                q0 = QB + m * (m - 1) // 2
                with pool.Fori(0, m) as k:
                    add(k + q0, NS - 1 - m, False)
                for c in range(2):
                    pool.wait_ge(added[c], q0 + m)
                pool.sem_inc(u_done, 1)

            pool.wait_ge(split_step, SPLIT_OPS * NS)
            def double(b, q):
                zb = U[:, bass.ds(b * P, P)]
                pool.tensor_tensor(zst[:, q, :], zb, zb, ALU.add).then_inc(z_staged, 1)

            for q in range(2):
                double(q, q)
            with pool.Fori(0, NB // 2 - 1) as g:
                for q in range(2):
                    pool.wait_ge(scores_done, g * (2 * NS) + NS * (q + 1))
                    double(g * 2 + (q + 2), q)

            pool.wait_ge(deg_step, 2)
            inverse_root(d2n[:, :], NB).then_inc(d2_ready, 1)

            pool.wait_ge(q_stored, 16 * NS)

            def gather(i, r, t):
                pool.wait_ge(gidx_ready, i * BS + r + 1)
                plain(pool)
                for k in range(TOPK):
                    pool.indirect_dma_start(G[:, t, k, :], None, q_dram,
                                            bass.IndirectOffsetOnAxis(ap=gidx[:, t, k:k + 1], axis=0)
                                            ).then_inc(g_sem[t], 16)

            with pool.Fori(0, NS) as i:
                q0 = i * NS + QC
                pool.wait_ge(ln_step, i * LN_OPS)
                pool.dma_start(xin, x_rows[bass.ds(i, 1), :, :, :].rearrange("i p b d -> (i p) b d")
                               ).then_inc(x_loaded, 16)
                gather(i, 0, 0)
                pool.wait_ge(turned, i)
                add(q0, 0, True)
                gather(i, 1, 1)
                with pool.Fori(1, BS // 2) as rr:
                    for t in range(2):
                        add(q0 + rr * 2 + (t - 1), 0, False)
                        gather(i, rr * 2 + t, t)
                add(q0 + (NS - 1), 0, False)
                pool.wait_ge(ln_step, i * LN_OPS + (LN_OPS - 1))
                inverse_root(stat[:, 3, :], BS).then_inc(rstd_ready, 1)
                pool.wait_ge(ln_step, (i + 1) * LN_OPS)
                plain(pool)
                pool.dma_start(out_rows[bass.ds(i, 1), :, :, :].rearrange("i p b d -> (i p) b d"),
                               osq).then_inc(out_stored, 16)
            pool.wait_ge(out_stored, 16 * NS)



def kernel(x, adj, L0_gnn_W1, L0_gnn_b1, L0_gnn_W2, L0_gnn_b2):
    import numpy as np
    import concourse.bacc as bacc
    from concourse.bass_utils import run_bass_kernel_spmd

    a = np.asarray(adj).reshape(NS, SB, NS, BS, P).transpose(0, 2, 4, 3, 1)
    tiles = np.empty((NS * NS, P, BS, SB), a.dtype)
    for i in range(NS):
        for r in range(NS):
            tiles[i * NS + r] = a[i, (i + 1 + r) % NS]
    x = np.ascontiguousarray(x)
    arrays = {
        "at": tiles,
        "xt": np.ascontiguousarray(x.T),
        "x": x,
        "w1": np.ascontiguousarray(L0_gnn_W1),
        "b1": np.ascontiguousarray(L0_gnn_b1).reshape(D, 1),
        "w2": np.ascontiguousarray(L0_gnn_W2),
        "b2": np.ascontiguousarray(L0_gnn_b2).reshape(1, D),
    }
    nc = bacc.Bacc("TRN2", target_bir_lowering=False, num_devices=1)
    ins = [nc.dram_tensor(name, a.shape, F32, kind="ExternalInput").ap() for name, a in arrays.items()]
    out = nc.dram_tensor("out", [N, D], F32, kind="ExternalOutput").ap()
    q_dram = nc.dram_tensor("q_dram", [N, D], F32).ap()
    gnn_kernel(nc, *ins, out, q_dram)
    r = run_bass_kernel_spmd(nc, [arrays], core_ids=[0])
    return r.results[0]["out"]
```

```python
from contextlib import ExitStack

import concourse.bass as bass
from concourse import mybir

P = 128
N = 8192
D = 128
NB = N // P
SB = 1024
NS = N // SB
BS = SB // P
CH = 512
HB = BS // 2
RING = 3
TOPK = 4
EPS_D2 = 1e-10
EPS_LN = 1e-5

ALU = mybir.AluOpType
ACT = mybir.ActivationFunctionType
AX = mybir.AxisListType
F32 = mybir.dt.float32
BF16 = mybir.dt.bfloat16
F32R = mybir.dt.float32r
U32 = mybir.dt.uint32

TILES_A = NS * NS
TILES_B = NS * (NS - 1) // 2
QB = NS * (NS + 1) // 2
QC = QB + TILES_B


def gnn_kernel(nc, at, xt, x, w12, b1, b2, out, q_dram, xw2_dram):
    with ExitStack() as ctx:
        def sb(name, shape, dt=F32):
            return ctx.enter_context(nc.sbuf_tensor(name, shape, dt))

        def sem(name):
            return ctx.enter_context(nc.semaphore(name))

        ring_at = -(-nc.sbuf_base // 32) * 32
        ring = sb("ring", [P, RING, BS, SB])
        Y = sb("Y", [P, NB, D])
        U = sb("U", [P, N])
        sqp = sb("sqp", [P, N], BF16)
        ystage_at = -(-nc.sbuf_base // 32) * 32
        ystage2 = sb("ystage2", [P, 2, 2, HB, D])
        ystage = ystage2[:, 0]
        part = sb("part", [P, 2, SB])
        rsum = sb("rsum", [P, SB])
        diag = sb("diag", [P, BS, P])
        ztmp = sb("ztmp", [P, CH])
        ident = sb("ident", [P, P])
        ones = sb("ones", [P, P])
        negsel = sb("negsel", [P, P], BF16)
        w12s = sb("w12s", [P, 2 * D])
        zeros = sb("zeros", [P, CH], BF16)
        b1s = sb("b1s", [P, 1])
        b2b = sb("b2b", [P, 1, D])
        rn = sb("rn", [P, NB])
        dn = sb("dn", [P, NB])
        sqn = sb("sqn", [P, NB])
        d2n = sb("d2n", [P, NB])
        mhalf = sb("mhalf", [P, NB])
        top8 = sb("top8", [P, 2, 8])
        idx8 = sb("idx8", [P, 2, 8], U32)
        gidx = sb("gidx", [P, 2, TOPK], U32)
        stat = sb("stat", [P, 4, BS])

        xt_all = U
        b2r = ztmp[0:1, 0:D]
        xw2s = diag.rearrange("p (q b) d -> p q (b d)", q=2)
        zsq, resid = part[:, 1, :], rsum
        xts = ystage2[:, 1].rearrange("p h b d -> p h (b d)")
        raw = ring[:, 1]
        a_hi = nc.alloc_sbuf_tensor_at("a_hi", [P, BS, SB], F32R, offset=ring_at + 2 * BS * SB * 4)
        a_lo = nc.alloc_sbuf_tensor_at("a_lo", [P, BS, SB], F32R, offset=ring_at)
        y_parts = nc.alloc_sbuf_tensor_at("y_parts", [P, 2, 2, HB, D], F32R, offset=ystage_at)
        rows = [ring[:, q, :, :].rearrange("p b i -> p (b i)") for q in (2, 0)]
        zst = rsum[:, 0:2 * P].rearrange("p (q i) -> p q i", q=2)
        topv = part[:, 0, 0:NB * TOPK].rearrange("p (b k) -> p b k", k=TOPK)
        S = part[:, 0, NB * TOPK:2 * NB * TOPK].rearrange("p (b k) -> p b k", k=TOPK)
        topi = part[:, 0, 2 * NB * TOPK:3 * NB * TOPK].bitcast(U32).rearrange("p (b k) -> p b k", k=TOPK)
        acc, xin, obuf, osq, gath = (U[:, t * SB:(t + 1) * SB] for t in (0, 3, 4, 5, 6))
        gsum = U[:, SB:3 * SB].rearrange("p (i b d) -> p i b d", i=2, d=D)
        xin, obuf, osq = (v.rearrange("p (b d) -> p b d", b=BS) for v in (xin, obuf, osq))
        G = gath.rearrange("p (q k d) -> p q k d", q=2, k=TOPK)

        ps = ctx.enter_context(nc.psum_tensor("ps", [P, 8, CH], F32))
        PROD, BC, SMALL = 0, 4, 6

        half_sem = [sem(f"half_sem{s}") for s in range(2 * RING)]
        half_loaded = sem("half_loaded")
        consts_in = sem("consts_in")
        xt_in = [sem(f"xt_in{q}") for q in range(2)]
        const_step = sem("const_step")
        neg_step = sem("neg_step")
        b2_done = sem("b2_done")
        b2_kept = sem("b2_kept")
        xts_ready = sem("xts_ready")
        proj_done = sem("proj_done")
        proj_kept = sem("proj_kept")
        xw2_stored = [sem(f"xw2_stored{q}") for q in range(2)]
        xw2_loaded = sem("xw2_loaded")
        staged = [sem(f"staged{h}") for h in range(2)]
        w_used = [sem(f"w_used{h}") for h in range(2)]
        quarter_sem = [sem(f"quarter_sem{k}") for k in range(4)]
        quarter_loaded = sem("quarter_loaded")
        hi_ready = sem("hi_ready")
        lo_ready = sem("lo_ready")
        lo_shared = sem("lo_shared")
        y_lo_ready = [sem(f"y_lo_ready{h}") for h in range(2)]
        parts_used = sem("parts_used")
        sum_done = sem("sum_done")
        sum_kept = sem("sum_kept")
        part_done = sem("part_done")
        row_step = sem("row_step")
        rnat_done = sem("rnat_done")
        rn_copied = sem("rn_copied")
        d_ready = sem("d_ready")
        diag_staged = sem("diag_staged")
        y_ready = sem("y_ready")
        diag_ready = sem("diag_ready")
        bc_done = sem("bc_done")
        z_step = sem("z_step")
        zsq_ready = sem("zsq_ready")
        sq_done = sem("sq_done")
        sqn_copied = sem("sqn_copied")
        split_step = sem("split_step")
        z_staged = sem("z_staged")
        scores_done = sem("scores_done")
        banks_free = sem("banks_free")
        max_done = sem("max_done")
        row_free = sem("row_free")
        top_kept = sem("top_kept")
        dist_step = sem("dist_step")
        root_done = sem("root_done")
        s_ready = sem("s_ready")
        deg_step = sem("deg_step")
        q_ready = sem("q_ready")
        q_stored = sem("q_stored")
        gidx_ready = sem("gidx_ready")
        g_sem = [sem(f"g_sem{q}") for q in range(2)]
        g_step = sem("g_step")
        turned = sem("turned")
        x_loaded = sem("x_loaded")
        ln_step = sem("ln_step")
        rstd_ready = sem("rstd_ready")
        out_stored = sem("out_stored")
        passed = sem("passed")

        Z_OPS, SPLIT_OPS, LN_OPS = 8, 5, 11
        SHARE = 1
        PARTS = 2 * NS - 1

        def products_before(n):
            if n >= TILES_A:
                return QB + n - TILES_A
            i, r = divmod(n, NS)
            return i * (i + 1) // 2 + max(0, r - (NS - 1 - i))

        def over(column, n):
            return column.rearrange("p (b a) -> p b a", a=1).to_broadcast([P, BS, n])

        def plain(engine):
            engine.sem_inc(passed, 1)

        x_rows = x.rearrange("(i b p) d -> i p b d", b=BS, p=P)
        out_rows = out.rearrange("(i b p) d -> i p b d", b=BS, p=P)

        block = ctx.enter_context(nc.Block())

        @block.sync
        def _(sp):
            for dst, src in ((w12s[:, :], w12), (b1s[:, :], b1), (b2r, b2)):
                sp.dma_start(dst, src).then_inc(consts_in, 16)
            for q in range(2):
                cols = slice(q * N // 2, (q + 1) * N // 2)
                sp.dma_start(xt_all[:, cols], xt[:, cols]).then_inc(xt_in[q], 16)

            def pass_on(slot, h, turn):
                sp.wait_ge(half_sem[2 * slot + h], turn * 16 + 16)
                sp.sem_inc(half_loaded, 1)

            def load(slot, h, tile):
                sp.dma_start(ring[:, slot, h * HB:(h + 1) * HB, :],
                             at[tile, :, h * HB:(h + 1) * HB, :]).then_inc(half_sem[2 * slot + h], 16)

            tiles = [(i, r) for i in range(NS) for r in range(NS)]
            for n, (i, r) in enumerate(tiles):
                for h in range(2):
                    if n:
                        pass_on((n - 1) % RING, h, (n - 1) // RING)
                    if n >= RING:
                        sp.wait_ge(part_done, min(2 * (n - RING) + h + 1, 2 * TILES_A))
                        if products_before(n - RING + 1):
                            sp.wait_ge(w_used[h], products_before(n - RING + 1))
                    load(n % RING, h, i * NS + r)
            for h in range(2):
                pass_on((TILES_A - 1) % RING, h, (TILES_A - 1) // RING)

            def pass_quarter(k, turn):
                sp.wait_ge(quarter_sem[k], turn * 16 + 16)
                sp.sem_inc(quarter_loaded, 1)

            def load_tile(u, tile, fresh=False):
                for k in range(4):
                    if not (fresh and k < 2):
                        pass_quarter((k - 2) % 4, u + (-1 if k < 2 else 0))
                    if isinstance(u, int) and u == 0:
                        sp.wait_ge(part_done, 2 * TILES_A - 4)
                        sp.wait_ge(w_used[1], products_before(TILES_A - 2))
                    else:
                        sp.wait_ge(hi_ready, u * 4 + (k - 3))
                        sp.wait_ge(lo_ready, u * 4 + (k - 3))
                        if k == 3:
                            sp.wait_ge(lo_shared, u)
                    sp.dma_start(raw[:, 2 * k:2 * k + 2, :], at[tile, :, 2 * k:2 * k + 2, :]).then_inc(quarter_sem[k], 16)

            load_tile(0, (NS - 2) * NS, True)
            for m in range(2, NS):
                u0 = m * (m - 1) // 2
                with sp.Fori(0, m) as r:
                    load_tile(r + u0, r + (NS - 1 - m) * NS)
            for k in (2, 3):
                pass_quarter(k, TILES_B - 1)

            for h in range(2):
                sp.wait_ge(staged[h], QC)
                sp.wait_ge(y_lo_ready[h], TILES_B)
                sp.wait_ge(xw2_stored[h], NB // HB // 2 * 16)
            sp.dma_start(Y.rearrange("p (s b) d -> p s (b d)", b=HB),
                         xw2_dram.rearrange("s p c -> p s c")).then_inc(xw2_loaded, 16)

            load_tile(TILES_B, 0, True)
            with sp.Fori(1, NS * NS) as c:
                load_tile(c + TILES_B, c)
            for k in (2, 3):
                pass_quarter(k, TILES_B + NS * NS - 1)

        @block.tensor
        def _(pe):
            def open_sums(row):
                if not (isinstance(row, int) and row < 2):
                    pe.wait_ge(sum_kept, row - 1)
                for c in range(2):
                    pe.matmul(ps[:, (row % 2) * 2 + c, :], zeros[:, 0:P], zeros[:, :], start=True, stop=False,
                              skip_group_check=True)

            def product(q, n, row, close=False):
                for c in range(2):
                    for b in range(BS):
                        if c == 0 and b % HB == 0:
                            pe.wait_ge(half_loaded, n * 2 + (1 + b // HB))
                            pe.wait_ge(staged[b // HB], q + 1)
                        mm = pe.matmul(ps[:, (row % 2) * 2 + c, :], ystage[:, b // HB, b % HB, :],
                                       ring[:, n % RING, b, c * CH:(c + 1) * CH],
                                       start=False, stop=(b == BS - 1), skip_group_check=True)
                        if c == 1 and b % HB == HB - 1:
                            mm.then_inc(w_used[b // HB], 1)

            def product_of_parts(q, row):
                u = q - QB if isinstance(q, int) else q + (-QB)
                for k in range(4):
                    h = k // 2
                    pe.wait_ge(hi_ready, u * 4 + (k + 1))
                    pe.wait_ge(lo_ready, u * 4 + (k + 1))
                    if k == 3:
                        pe.wait_ge(lo_shared, u + 1)
                    if k % 2 == 0:
                        pe.wait_ge(staged[h], q + 1)
                        pe.wait_ge(y_lo_ready[h], u + 1)
                    for c in range(2):
                        for b in (2 * k, 2 * k + 1):
                            for y, a in ((0, a_hi), (0, a_lo), (1, a_hi)):
                                mm = pe.matmul(ps[:, (row % 2) * 2 + c, :], y_parts[:, h, y, b % HB, :],
                                               a[:, b, c * CH:(c + 1) * CH],
                                               start=False, stop=(k == 3 and b == BS - 1 and y == 1),
                                               skip_group_check=True)
                    mm.then_inc(parts_used, 1)

            def close_sums(q, of_parts=True):
                if not of_parts:
                    pe.wait_ge(w_used[1], q + 1)
                else:
                    pe.wait_ge(parts_used, (q + (1 - QB)) * 4)
                pe.sem_inc(sum_done, 1)

            def spread_d(f):
                pe.wait_ge(diag_ready, f + 1)
                if f:
                    pe.wait_ge(split_step, SPLIT_OPS * f)
                for c in range(2):
                    mm = pe.matmul(ps[:, BC + c, :], ones[:, :],
                                   diag[:, c * HB:(c + 1) * HB, :].rearrange("p b i -> p (b i)"),
                                   start=True, stop=True)
                mm.then_inc(bc_done, 1)

            def squares(f):
                pe.wait_ge(zsq_ready, f + 1)
                if f:
                    pe.wait_ge(sqn_copied, f)
                for c in range(2):
                    pe.matmul(ps[:, BC + c, :], ones[:, :], zsq[:, c * CH:(c + 1) * CH], start=True, stop=True)
                for b in range(BS):
                    mm = pe.matmul(ps[:, SMALL, b:b + 1], zsq[:, b * P:(b + 1) * P], ones[:, 0:1],
                                   start=True, stop=True)
                mm.then_inc(sq_done, 1)

            pe.wait_ge(const_step, 5)
            pe.wait_ge(consts_in, 48)
            pe.matmul(ps[:, SMALL, 0:D], ones[0:1, :], b2r, start=True, stop=True).then_inc(b2_done, 1)
            with pe.Fori(0, NB // HB // 2) as g:
                for q in range(2):
                    pe.wait_ge(xts_ready, g * 2 + (q + 1))
                    pe.wait_ge(proj_kept, g * 4 + 2 * q)
                    for b in range(HB):
                        mm = pe.matmul(ps[:, 2 * q + b // 2, (b % 2) * 2 * D:(b % 2 + 1) * 2 * D],
                                       xts[:, q, b * P:(b + 1) * P], w12s[:, :], start=True, stop=True)
                    mm.then_inc(proj_done, 1)
            pe.wait_ge(proj_kept, 2 * NB // HB)
            pe.wait_ge(b2_kept, 1)
            for i in range(NS):
                q0 = i * (i + 1) // 2
                open_sums(i)
                if i:
                    with pe.Fori(0, i) as k:
                        product(k + q0, k + (NS * i + NS - 1 - i), i)
                pe.wait_ge(row_step, PARTS * (i + 1))
                if i:
                    pe.wait_ge(rn_copied, i)
                pe.matmul(ps[:, SMALL, 0:BS], zeros[:, 0:P], zeros[:, 0:BS], start=True, stop=False,
                          skip_group_check=True)
                for v in (rsum[:, :], part[:, 1, :]):
                    for b in range(BS):
                        mm = pe.matmul(ps[:, SMALL, b:b + 1], v[:, b * P:(b + 1) * P], ones[:, 0:1],
                                       start=False, stop=True, skip_group_check=True)
                    pe.wait_ge(part_done, 2 * NS * (i + 1))
                mm.then_inc(rnat_done, 1)
                product(q0 + i, NS * i + NS - 1, i)
                close_sums(q0 + i, False)
            spread_d(0)
            pe.wait_ge(rn_copied, NS)
            for m in range(1, NS):
                q0 = QB + m * (m - 1) // 2
                row = NS - 1 + m
                open_sums(row)
                product_of_parts(q0, row)
                squares(m - 1)
                if m > 1:
                    with pe.Fori(1, m) as k:
                        product_of_parts(k + q0, row)
                close_sums(q0 + m - 1)
                spread_d(m)
            squares(NS - 1)

            pe.wait_ge(split_step, SPLIT_OPS * NS)
            with pe.Fori(0, NB // 2) as g:
                for q in range(2):
                    pe.wait_ge(z_staged, g * 2 + (q + 1))
                    for cc in range(NS):
                        pair = 2 * (cc % 2)
                        pe.wait_ge(banks_free, g * (2 * NS) + (NS * q + cc + 1))
                        for c in range(2):
                            cols = slice((2 * cc + c) * CH, (2 * cc + c + 1) * CH)
                            pe.matmul(ps[:, pair + c, :], zst[:, q, :], U[:, cols], start=True, stop=False)
                            mm = pe.matmul(ps[:, pair + c, :], negsel[:, :], sqp[:, cols], start=False, stop=True)
                        mm.then_inc(scores_done, 1)

            def turn(i):
                pe.wait_ge(sum_kept, i + (2 * NS))
                pe.wait_ge(ln_step, i * LN_OPS)
                for b in range(BS):
                    mm = pe.transpose(ps[:, BC + b // HB, (b % HB) * P:(b % HB + 1) * P],
                                      acc[:, b * P:(b + 1) * P], ident[:, :])
                mm.then_inc(turned, 1)

            pe.wait_ge(banks_free, 2 + NS * NB)

            def row_c(i, later):
                row = i + (2 * NS - 1)
                open_sums(row)
                product_of_parts(i * NS + QC, row)
                if later:
                    turn(i - 1)
                with pe.Fori(1, NS) as r:
                    product_of_parts(i * NS + r + QC, row)
                close_sums(i * NS + (QC + NS - 1))

            row_c(0, False)
            with pe.Fori(1, NS) as i:
                row_c(i, True)
            turn(NS - 1)

        @block.scalar
        def _(act):
            def stage(q, j):
                for h in range(2):
                    if not (isinstance(q, int) and q == 0):
                        act.wait_ge(w_used[h], q)
                    act.activation(ystage[:, h, :, :], Y[:, bass.ds(j * BS + h * HB, HB), :],
                                   ACT.Copy).then_inc(staged[h], 1)

            def stage_scaled(q, j):
                act.wait_ge(d_ready, j + 1)
                for h in range(2):
                    if q:
                        act.wait_ge(w_used[h], q)
                    for b in range(HB):
                        blk = j * BS + h * HB + b
                        ins = act.activation(ystage[:, h, b, :], Y[:, blk, :], ACT.Copy, scale=dn[:, blk:blk + 1])
                    ins.then_inc(staged[h], 1)
                act.wait_ge(staged[1], q + 1)
                act.sem_inc(diag_staged, 1)

            def first_parts(q, j):
                u = q - QB if isinstance(q, int) else q + (-QB)
                for h in range(2):
                    if isinstance(u, int) and u == 0:
                        act.wait_ge(w_used[h], q)
                    else:
                        act.wait_ge(parts_used, u * 4 + (2 * h - 2))
                    act.activation(y_parts[:, h, 0, :, :], Y[:, bass.ds(j * BS + h * HB, HB), :],
                                   ACT.Copy).then_inc(staged[h], 1)
                    for k in (2 * h, 2 * h + 1):
                        act.wait_ge(quarter_loaded, u * 4 + (k + 1))
                        if not (isinstance(u, int) and u == 0):
                            act.wait_ge(parts_used, u * 4 + (k - 3))
                        act.activation(a_hi[:, 2 * k:2 * k + 2, :], raw[:, 2 * k:2 * k + 2, :],
                                       ACT.Copy).then_inc(hi_ready, 1)

            act.wait_ge(b2_done, 1)
            act.activation(b2b[:, 0, :], ps[:, SMALL, 0:D], ACT.Copy).then_inc(b2_kept, 1)

            def feed_xt(s, q):
                act.activation(xts[:, q, :], xt_all[:, bass.ds(s * CH, CH)], ACT.Copy).then_inc(xts_ready, 1)

            for q in range(2):
                act.wait_ge(xt_in[q], 16)
            for q in range(2):
                feed_xt(q, q)
            with act.Fori(0, NB // HB // 2) as g:
                for q in range(2):
                    both = ps[:, 2 * q:2 * q + 2, :].rearrange("p c (b w d) -> p (c b) w d", w=2, d=D)
                    act.wait_ge(proj_done, g * 2 + (q + 1))
                    act.activation(Y[:, bass.ds((g * 2 + q) * HB, HB), :], both[:, :, 0, :],
                                   ACT.Copy).then_inc(proj_kept, 1)
                    act.wait_ge(xw2_stored[q], g * 16)
                    act.activation(xw2s[:, q, :].rearrange("p (b d) -> p b d", d=D), both[:, :, 1, :],
                                   ACT.Copy).then_inc(proj_kept, 1)
                    feed_xt((g * 2 + (q + 2)) % (NB // HB), q)
                    act.wait_ge(proj_kept, g * 4 + (2 * q + 2))
                    act.dma_start(xw2_dram[bass.ds(g * 2 + q, 1), :, :].rearrange("s p c -> (s p) c"),
                                  xw2s[:, q, :]).then_inc(xw2_stored[q], 16)

            act.wait_ge(xts_ready, NB // HB + 2)
            for i in range(NS):
                q0 = i * (i + 1) // 2
                if i > 1:
                    with act.Fori(1, i) as k:
                        stage(k + q0, k)
                act.wait_ge(rnat_done, i + 1)
                act.activation(rn[:, i * BS:(i + 1) * BS], ps[:, SMALL, 0:BS], ACT.Copy).then_inc(rn_copied, 1)
                stage_scaled(q0 + i, i)
                act.wait_ge(y_ready, i + 1)
                if i < NS - 1:
                    stage(q0 + i + 1, 0)
                act.wait_ge(sum_done, i + 1)
                act.activation(U[:, i * SB:(i + 1) * SB].rearrange("p (c i) -> p c i", c=2),
                               ps[:, 2 * (i % 2):2 * (i % 2) + 2, :], ACT.Copy).then_inc(sum_kept, 1)

            def square(f):
                act.wait_ge(z_step, Z_OPS * (f + 1))
                if f:
                    act.wait_ge(sq_done, f)
                act.activation(zsq, U[:, (NS - 1 - f) * SB:(NS - f) * SB],
                               ACT.Square).then_inc(zsq_ready, 1)

            def keep_squares(f):
                act.wait_ge(sq_done, f + 1)
                act.activation(sqn[:, (NS - 1 - f) * BS:(NS - f) * BS], ps[:, SMALL, 0:BS],
                               ACT.Copy).then_inc(sqn_copied, 1)

            for m in range(1, NS):
                q0 = QB + m * (m - 1) // 2
                first_parts(q0, NS - m)
                square(m - 1)
                if m > 1:
                    with act.Fori(1, m) as k:
                        first_parts(k + q0, k + (NS - m))
                keep_squares(m - 1)
            square(NS - 1)
            keep_squares(NS - 1)

            act.wait_ge(split_step, SPLIT_OPS * NS)
            act.wait_ge(sum_kept, 2 * NS - 1)
            act.sem_inc(banks_free, 2)
            with act.Fori(0, NB // 2) as g:
                for q in range(2):
                    act.wait_ge(row_free, g * 2 + (q + 1))
                    for cc in range(NS):
                        act.wait_ge(scores_done, g * (2 * NS) + (NS * q + cc + 1))
                        act.activation(rows[q][:, cc * SB:(cc + 1) * SB],
                                       ps[:, 2 * (cc % 2):2 * (cc % 2) + 2, :].rearrange("p c i -> p (c i)"),
                                       ACT.Copy).then_inc(banks_free, 1)

            act.wait_ge(dist_step, 2)
            act.activation(S, topv, ACT.Sqrt).then_inc(root_done, 1)
            act.wait_ge(root_done, 1)
            act.activation(S, S, ACT.Exp, scale=-0.5).then_inc(s_ready, 1)

            act.wait_ge(deg_step, 2)
            act.activation(d2n[:, :], d2n[:, :], ACT.Sqrt).then_inc(root_done, 1)

            def keep_sums(i):
                act.wait_ge(sum_done, i + (2 * NS))
                act.wait_ge(turned, i)
                act.activation(acc.rearrange("p (c i) -> p c i", c=2),
                               ps[:, bass.ds(((i + 1) % 2) * 2, 2), :], ACT.Copy).then_inc(sum_kept, 1)

            with act.Fori(0, NS) as r:
                act.wait_ge(q_ready, r + 1)
                first_parts(r + QC, (r + 1) % NS)
            with act.Fori(1, NS) as i:
                first_parts(i * NS + QC, (i + 1) % NS)
                keep_sums(i - 1)
                with act.Fori(1, NS) as r:
                    first_parts(i * NS + r + QC, (i + 1 + r) % NS)
            keep_sums(NS - 1)

        @block.vector
        def _(dve):
            def sum_half(n, h):
                dve.wait_ge(half_loaded, n * 2 + (h + 1))
                dve.tensor_reduce(part[:, h, :],
                                  ring[:, n % RING, h * HB:(h + 1) * HB, :].rearrange("p b i -> p i b"),
                                  AX.X, ALU.add).then_inc(part_done, 1)

            with dve.Fori(0, NS) as i:
                dve.wait_ge(row_step, i * PARTS)
                sum_half(i * NS, 0)
                dve.wait_ge(rnat_done, i)
                sum_half(i * NS, 1)
                with dve.Fori(0, NS - 1) as r:
                    for h in range(2):
                        dve.wait_ge(row_step, i * PARTS + r * 2 + (h + 1))
                        sum_half(i * NS + r + 1, h)

            dve.wait_ge(rnat_done, NS)
            dve.wait_ge(b2_done, 1)

            def second_parts(u):
                for k in range(4):
                    blocks = slice(2 * k, min(2 * k + 2, BS - SHARE))
                    dve.wait_ge(hi_ready, u * 4 + (k + 1))
                    dve.tensor_tensor(a_lo[:, blocks, :], raw[:, blocks, :], a_hi[:, blocks, :].bitcast(F32),
                                      ALU.subtract).then_inc(lo_ready, 1)

            def finish(f, fresh):
                sup = (f * (NS - 1) + (NS - 1)) % NS

                def z_op(k, instruction):
                    instruction.then_inc(z_step, 1)
                    dve.wait_ge(z_step, f * Z_OPS + (k + 1))

                dve.wait_ge(bc_done, f + 1)
                dve.wait_ge(sum_kept, NS)
                for c in range(2):
                    u = U[:, bass.ds(sup * SB + c * CH, CH)]
                    if fresh:
                        z_op(4 * c, dve.tensor_copy(ztmp[:, :], u))
                    else:
                        dve.wait_ge(sum_done, f + NS)
                        z_op(4 * c, dve.tensor_tensor(ztmp[:, :], u, ps[:, ((f + 1) % 2) * 2 + c, :], ALU.add))
                        if c == 1:
                            dve.sem_inc(sum_kept, 1)
                    z_op(4 * c + 1, dve.tensor_tensor(ztmp[:, :], ztmp[:, :], ps[:, BC + c, :], ALU.mult))
                    z_op(4 * c + 2, dve.tensor_scalar(ztmp[:, :], ztmp[:, :], b1s[:, :], None, ALU.add))
                    z_op(4 * c + 3, dve.scalar_tensor_tensor(out=u, in0=ztmp[:, :], scalar=0.1, in1=ztmp[:, :],
                                                             op0=ALU.mult, op1=ALU.max))

            def split(f):
                sup = (f * (NS - 1) + (NS - 1)) % NS
                dve.wait_ge(sq_done, f + 1)
                sq = ps[:, BC:BC + 2, :].rearrange("p c i -> p (c i)")
                cols = bass.ds(sup * SB, SB)
                dve.tensor_copy(sqp[:, cols], sq).then_inc(split_step, 1)
                for t, p0 in enumerate((64, 96)):
                    dve.wait_ge(split_step, f * SPLIT_OPS + (2 * t + 1))
                    dve.tensor_tensor(resid[p0:P, :], sq[p0:P, :] if t == 0 else resid[p0:P, :],
                                      sqp[p0:P, cols], ALU.subtract).then_inc(split_step, 1)
                    dve.wait_ge(split_step, f * SPLIT_OPS + (2 * t + 2))
                    plain(dve)
                    dve.tensor_copy(sqp[p0:P, cols], resid[p0:P, :]).then_inc(split_step, 1)

            for m in range(1, NS):
                u0 = m * (m - 1) // 2
                second_parts(u0)
                finish(m - 1, m == 1)
                if m > 1:
                    second_parts(u0 + 1)
                split(m - 1)
                if m > 2:
                    with dve.Fori(2, m) as r:
                        second_parts(r + u0)
            finish(NS - 1, False)
            split(NS - 1)

            dve.wait_ge(sq_done, NS)
            dve.sem_inc(row_free, 2)

            def best(b, q, g):
                dve.wait_ge(banks_free, g * (2 * NS) + (NS * (q + 1) + 2))
                plain(dve)
                dve.max(top8[:, q, :], rows[q]).then_inc(max_done, 1)

            def find(b, q):
                dve.wait_ge(max_done, b + 1)
                plain(dve)
                dve.max_index(idx8[:, q, :], top8[:, q, :], rows[q]).then_inc(row_free, 1)

            def keep(b, q):
                dve.wait_ge(row_free, b + 3)
                dve.tensor_copy(topv[:, bass.ds(b, 1), :], top8[:, q:q + 1, 0:TOPK]).then_inc(top_kept, 1)
                dve.tensor_copy(topi[:, bass.ds(b, 1), :], idx8[:, q:q + 1, 0:TOPK]).then_inc(top_kept, 1)

            best(0, 0, 0)
            find(0, 0)
            best(1, 1, 0)
            keep(0, 0)
            find(1, 1)
            with dve.Fori(1, NB // 2) as g:
                for q in range(2):
                    dve.wait_ge(top_kept, g * 4 + (2 * q - 2))
                    best(g * 2 + q, q, g)
                    keep(g * 2 + (q - 1), 1 - q)
                    find(g * 2 + q, q)
            keep(NB - 1, 1)

            dve.wait_ge(top_kept, 2 * NB)
            dve.wait_ge(sqn_copied, NS)
            dve.tensor_tensor(topv, sqn.rearrange("p (b a) -> p b a", a=1).to_broadcast([P, NB, TOPK]), topv,
                              ALU.subtract).then_inc(dist_step, 1)
            dve.wait_ge(dist_step, 1)
            dve.tensor_scalar(topv, topv, 0.0, EPS_D2, ALU.max, ALU.add).then_inc(dist_step, 1)
            dve.wait_ge(s_ready, 1)
            dve.tensor_reduce(d2n[:, :], S, AX.X, ALU.add).then_inc(deg_step, 1)
            dve.wait_ge(deg_step, 1)
            dve.tensor_tensor(d2n[:, :], d2n[:, :], rn[:, :], ALU.add).then_inc(deg_step, 1)
            dve.wait_ge(root_done, 2)
            dve.reciprocal(d2n[:, :], d2n[:, :]).then_inc(deg_step, 1)
            dve.wait_ge(deg_step, 3)
            dve.wait_ge(xw2_loaded, 16)
            for j in [*range(1, NS), 0]:
                yj = Y[:, j * BS:(j + 1) * BS, :]
                dve.tensor_tensor(yj, yj, over(d2n[:, j * BS:(j + 1) * BS], D), ALU.mult).then_inc(q_ready, 1)

            dve.tensor_copy(gidx[:, 0, :], topi[:, 0, :]).then_inc(gidx_ready, 1)

            def weighted_sum(row, col, blk, t, n):
                dve.wait_ge(g_sem[t], n * (16 * TOPK))
                gs = gsum[:, row % 2, bass.ds(col, 1), :].rearrange("p a d -> p (a d)")
                for k in range(TOPK):
                    sk = S[:, bass.ds(blk, 1), k:k + 1].rearrange("p a k -> p (a k)")
                    if k == 0:
                        dve.tensor_scalar(gs, G[:, t, k, :], sk, None, ALU.mult).then_inc(g_step, 1)
                    else:
                        dve.wait_ge(g_step, blk * TOPK + k)
                        dve.scalar_tensor_tensor(out=gs, in0=G[:, t, k, :], scalar=sk, in1=gs,
                                                 op0=ALU.mult, op1=ALU.add).then_inc(g_step, 1)

            def pair(i, rr, first=False, between=()):
                for t in range(2):
                    blk = i * BS + rr * 2 + t
                    second_parts(blk + TILES_B)
                    if t == 1:
                        weighted_sum(i, rr * 2, blk - 1, 0, i * HB + rr + 1)
                    elif isinstance(rr, int) and rr == 0:
                        if not first:
                            weighted_sum(i + 1, BS - 1, blk - 1, 1, i * HB)
                    else:
                        weighted_sum(i, rr * 2 - 1, blk - 1, 1, i * HB + rr)
                    if not (first and t == 0):
                        dve.wait_ge(g_step, blk * TOPK)
                    dve.tensor_copy(gidx[:, 1 - t:2 - t, :],
                                    topi[:, bass.ds((blk + 1) % NB, 1), :]).then_inc(gidx_ready, 1)
                    for step in between[t:t + 1]:
                        step(i - 1)

            def ln(i, steps):
                for n, step in steps:
                    if n:
                        dve.wait_ge(ln_step, i * LN_OPS + n)
                    step().then_inc(ln_step, 1)

            def residual(i):
                dve.wait_ge(turned, i + 1)
                ln(i, [(0, lambda: dve.tensor_tensor(obuf.rearrange("p b d -> p (b d)"),
                                                     ps[:, BC:BC + 2, :].rearrange("p c i -> p (c i)"),
                                                     gsum[:, i % 2, :, :].rearrange("p b d -> p (b d)"), ALU.add)),
                       (1, lambda: dve.tensor_tensor(obuf, obuf, over(d2n[:, bass.ds(i * BS, BS)], D), ALU.mult))])

            def add_x(i):
                dve.wait_ge(x_loaded, (i + 1) * 16)
                ln(i, [(2, lambda: dve.tensor_tensor(xin, xin, b2b[:, :, :].to_broadcast([P, BS, D]), ALU.add)),
                       (3, lambda: dve.tensor_tensor(obuf, obuf, xin, ALU.add))])

            def centre(i):
                ln(i, [(4, lambda: dve.tensor_reduce(stat[:, 0, :], obuf, AX.X, ALU.add)),
                       (5, lambda: dve.tensor_scalar(stat[:, 1, :], stat[:, 0, :], 1.0 / D, None, ALU.mult)),
                       (6, lambda: dve.tensor_tensor(obuf, obuf, over(stat[:, 1, :], D), ALU.subtract))])

            def variance(i):
                dve.wait_ge(out_stored, i * 16)
                ln(i, [(7, lambda: dve.tensor_tensor(osq, obuf, obuf, ALU.mult)),
                       (8, lambda: dve.tensor_reduce(stat[:, 2, :], osq, AX.X, ALU.add)),
                       (9, lambda: dve.tensor_scalar(stat[:, 3, :], stat[:, 2, :], 1.0 / D, EPS_LN,
                                                     ALU.mult, ALU.add))])

            def scale_row(i):
                dve.wait_ge(rstd_ready, i + 1)
                dve.wait_ge(ln_step, i * LN_OPS + (LN_OPS - 1))
                dve.tensor_tensor(osq, obuf, over(stat[:, 3, :], D), ALU.mult).then_inc(ln_step, 1)

            pair(0, 0, True)
            with dve.Fori(1, HB) as rr:
                pair(0, rr)
            with dve.Fori(1, NS) as i:
                pair(i, 0, between=(lambda _: None, residual))
                pair(i, 1, between=(add_x, centre))
                pair(i, 2, between=(variance,))
                pair(i, 3, between=(scale_row,))
            weighted_sum(NS + 1, BS - 1, NB - 1, 1, NS * HB)
            dve.wait_ge(g_step, NB * TOPK)
            for step in (residual, add_x, centre, variance, scale_row):
                step(NS - 1)

        @block.gpsimd
        def _(pool):
            pool.memset(ident[:, :], 0.0).then_inc(const_step, 1)
            pool.memset(ones[:, :], 1.0).then_inc(const_step, 1)
            pool.memset(mhalf[:, :], -0.5).then_inc(const_step, 1)
            pool.memset(negsel[:, :], 0.0).then_inc(const_step, 1)
            pool.memset(zeros[:, :], 0.0).then_inc(const_step, 1)
            pool.wait_ge(const_step, 5)
            pool.affine_select(out=ident[:, :], in_=ident[:, :], compare_op=ALU.not_equal, fill=1.0, base=0,
                               pattern=[[-1, P]], channel_multiplier=1).then_inc(neg_step, 1)
            for t, p0 in enumerate((0, 64, 96)):
                pool.wait_ge(neg_step, t + 1)
                pool.memset(negsel[p0:p0 + 1, :], -1.0).then_inc(neg_step, 1)
            pool.wait_ge(neg_step, 4)

            def make_diag(f):
                if f:
                    pool.wait_ge(bc_done, f)
                j = NS - 1 - f
                pool.tensor_tensor(diag[:, :, :],
                                   ident[:, :].rearrange("p (a i) -> p a i", a=1).to_broadcast([P, BS, P]),
                                   over(dn[:, j * BS:(j + 1) * BS], P), ALU.mult).then_inc(diag_ready, 1)

            with pool.Fori(0, NS) as i:
                def add_part(done, s, fresh, h):
                    pool.wait_ge(part_done, done)
                    if fresh:
                        plain(pool)
                        pool.tensor_copy(rsum[:, :], part[:, h, :]).then_inc(row_step, 1)
                    else:
                        pool.wait_ge(row_step, s)
                        pool.tensor_tensor(rsum[:, :], rsum[:, :], part[:, h, :], ALU.add).then_inc(row_step, 1)

                pool.wait_ge(rnat_done, i)
                add_part(i * (2 * NS) + 1, i * PARTS, True, 0)
                with pool.Fori(0, NS - 1) as r:
                    add_part(i * (2 * NS) + r * 2 + 2, i * PARTS + r * 2 + 1, False, 1)
                    add_part(i * (2 * NS) + r * 2 + 3, i * PARTS + r * 2 + 2, False, 0)

                pool.wait_ge(rn_copied, i + 1)
                cols = bass.ds(i * BS, BS)
                pool.tensor_tensor(dn[:, cols], rn[:, cols], mhalf[:, 0:BS], ALU.pow).then_inc(d_ready, 1)
                pool.wait_ge(d_ready, i + 1)
                pool.wait_ge(diag_staged, i + 1)
                pool.tensor_tensor(Y[:, cols, :], Y[:, cols, :], over(dn[:, cols], D), ALU.mult).then_inc(y_ready, 1)

            pool.wait_ge(xw2_stored[0], NB // HB // 2 * 16)
            pool.wait_ge(xw2_stored[1], NB // HB // 2 * 16)

            def second_share(q, j, between=()):
                u = q - QB if isinstance(q, int) else q + (-QB)
                for h in range(2):
                    pool.wait_ge(staged[h], q + 1)
                    pool.tensor_tensor(y_parts[:, h, 1, :, :], Y[:, bass.ds(j * BS + h * HB, HB), :], y_parts[:, h, 0, :, :].bitcast(F32),
                                       ALU.subtract).then_inc(y_lo_ready[h], 1)
                    for gather_one in between[2 * h:2 * h + 2]:
                        gather_one()
                pool.wait_ge(hi_ready, u * 4 + 4)
                blocks = slice(BS - SHARE, BS)
                pool.tensor_tensor(a_lo[:, blocks, :], raw[:, blocks, :], a_hi[:, blocks, :].bitcast(F32),
                                   ALU.subtract).then_inc(lo_shared, 1)

            make_diag(0)
            for m in range(1, NS):
                q0 = QB + m * (m - 1) // 2
                second_share(q0, NS - m)
                make_diag(m)
                if m > 1:
                    with pool.Fori(1, m) as k:
                        second_share(k + q0, k + (NS - m))

            pool.wait_ge(split_step, SPLIT_OPS * NS)
            def double(b, q):
                zb = U[:, bass.ds(b * P, P)]
                pool.tensor_tensor(zst[:, q, :], zb, zb, ALU.add).then_inc(z_staged, 1)

            for q in range(2):
                double(q, q)
            with pool.Fori(0, NB // 2 - 1) as g:
                for q in range(2):
                    pool.wait_ge(scores_done, g * (2 * NS) + NS * (q + 1))
                    double(g * 2 + (q + 2), q)

            for t, j in enumerate([*range(1, NS), 0]):
                pool.wait_ge(q_ready, t + 1)
                pool.dma_start(q_dram[j * SB:(j + 1) * SB, :].rearrange("(b p) d -> p b d", p=P),
                               Y[:, j * BS:(j + 1) * BS, :]).then_inc(q_stored, 16)

            pool.wait_ge(q_stored, 16 * NS)

            def tile_and_block(i, r, t):
                def gather(k):
                    if k == 0:
                        pool.wait_ge(gidx_ready, i * BS + r + 1)
                        plain(pool)
                    pool.indirect_dma_start(G[:, t, k, :], None, q_dram,
                                            bass.IndirectOffsetOnAxis(ap=gidx[:, t, k:k + 1], axis=0)
                                            ).then_inc(g_sem[t], 16)

                second_share(i * NS + r + QC, (i + r + 1) % NS,
                             [lambda k=k: gather(k) for k in range(TOPK)])

            def load_x(i):
                pool.wait_ge(ln_step, i * LN_OPS)
                plain(pool)
                pool.dma_start(xin, x_rows[bass.ds(i, 1), :, :, :].rearrange("i p b d -> (i p) b d")
                               ).then_inc(x_loaded, 16)

            def root(i):
                pool.wait_ge(ln_step, i * LN_OPS + (LN_OPS - 1))
                pool.tensor_tensor(stat[:, 3, :], stat[:, 3, :], mhalf[:, 0:BS], ALU.pow).then_inc(rstd_ready, 1)

            def store(i):
                pool.wait_ge(ln_step, (i + 1) * LN_OPS)
                plain(pool)
                pool.dma_start(out_rows[bass.ds(i, 1), :, :, :].rearrange("i p b d -> (i p) b d"),
                               osq).then_inc(out_stored, 16)

            load_x(0)
            with pool.Fori(0, BS // 2) as rr:
                for t in range(2):
                    tile_and_block(0, rr * 2 + t, t)
            with pool.Fori(1, NS) as i:
                for r in range(BS):
                    tile_and_block(i, r, r % 2)
                    if r == 4:
                        root(i - 1)
                store(i - 1)
                load_x(i)
            root(NS - 1)
            store(NS - 1)
            pool.wait_ge(out_stored, 16 * NS)



def kernel(x, adj, L0_gnn_W1, L0_gnn_b1, L0_gnn_W2, L0_gnn_b2):
    import numpy as np
    import concourse.bacc as bacc
    from concourse.bass_utils import run_bass_kernel_spmd

    a = np.asarray(adj).reshape(NS, SB, NS, BS, P).transpose(0, 2, 4, 3, 1)
    tiles = np.empty((NS * NS, P, BS, SB), a.dtype)
    for i in range(NS):
        for r in range(NS):
            tiles[i * NS + r] = a[i, (i + 1 + r) % NS]
    x = np.ascontiguousarray(x)
    arrays = {
        "at": tiles,
        "xt": np.ascontiguousarray(x.T),
        "x": x,
        "w12": np.concatenate([np.asarray(L0_gnn_W1), np.asarray(L0_gnn_W2)], axis=1),
        "b1": np.ascontiguousarray(L0_gnn_b1).reshape(D, 1),
        "b2": np.ascontiguousarray(L0_gnn_b2).reshape(1, D),
    }
    nc = bacc.Bacc("TRN2", target_bir_lowering=False, num_devices=1)
    ins = [nc.dram_tensor(name, a.shape, F32, kind="ExternalInput").ap() for name, a in arrays.items()]
    out = nc.dram_tensor("out", [N, D], F32, kind="ExternalOutput").ap()
    q_dram = nc.dram_tensor("q_dram", [N, D], F32).ap()
    xw2_dram = nc.dram_tensor("xw2_dram", [NB // HB, P, HB * D], F32).ap()
    gnn_kernel(nc, *ins, out, q_dram, xw2_dram)
    r = run_bass_kernel_spmd(nc, [arrays], core_ids=[0])
    return r.results[0]["out"]
```

```python
from contextlib import ExitStack

import concourse.bass as bass
from concourse import mybir

P = 128
N = 8192
D = 128
NB = N // P
SB = 1024
NS = N // SB
BS = SB // P
HP = P // 2
HSB = SB // 2
CH = 512
HB = BS // 2
RING = 3
TOPK = 4
EPS_D2 = 1e-10
EPS_LN = 1e-5

ALU = mybir.AluOpType
ACT = mybir.ActivationFunctionType
AX = mybir.AxisListType
F32 = mybir.dt.float32
BF16 = mybir.dt.bfloat16
F32R = mybir.dt.float32r
U32 = mybir.dt.uint32

TILES_A = NS * NS
TILES_B = NS * (NS - 1) // 2
QB = NS * (NS + 1) // 2
QC = QB + TILES_B


def gnn_kernel(nc, at, xt, x, w12, b1, b2, out, q_dram, xw2_dram, z_dram):
    with ExitStack() as ctx:
        def sb(name, shape, dt=F32):
            return ctx.enter_context(nc.sbuf_tensor(name, shape, dt))

        def sem(name):
            return ctx.enter_context(nc.semaphore(name))

        ring_at = -(-nc.sbuf_base // 32) * 32
        ring = sb("ring", [P, RING, BS, SB])
        Y = sb("Y", [P, NB, D])
        U_at = -(-nc.sbuf_base // 32) * 32
        U = sb("U", [P, N])
        sqp = sb("sqp", [P, N], BF16)
        ystage_at = -(-nc.sbuf_base // 32) * 32
        ystage2 = sb("ystage2", [P, 2, 2, HB, D])
        ystage = ystage2[:, 0]
        part = sb("part", [P, 2, SB])
        rsum_at = -(-nc.sbuf_base // 32) * 32
        rsum = sb("rsum", [P, SB])
        diag = sb("diag", [P, BS, P])
        ztmp = sb("ztmp", [P, CH])
        ident = sb("ident", [P, P])
        ones = sb("ones", [P, P])
        negsel = sb("negsel", [P, P], BF16)
        w12s = sb("w12s", [P, 2 * D])
        zeros = sb("zeros", [P, CH], BF16)
        b1s = sb("b1s", [P, 1])
        b2b = sb("b2b", [P, 1, D])
        rn = sb("rn", [P, NB])
        dn = sb("dn", [P, NB])
        d2n = sb("d2n", [P, NB])
        mhalf = sb("mhalf", [P, NB])
        top8 = sb("top8", [P, 2, 8])
        idx8 = sb("idx8", [P, 2, 8], U32)
        gidx = sb("gidx", [P, 2, TOPK], U32)
        stat = sb("stat", [P, 4, BS])
        ncand = sb("ncand", [P, 2 * TOPK])

        xt_all = U
        b2r = ztmp[0:1, 0:D]
        xw2s = diag.rearrange("p (q b) d -> p q (b d)", q=2)
        zsq, resid = part[:, 1, :], rsum
        xts = ystage2[:, 1].rearrange("p h b d -> p h (b d)")
        raw = ring[:, 1]
        a_hi = nc.alloc_sbuf_tensor_at("a_hi", [P, BS, SB], F32R, offset=ring_at)
        a_lo = nc.alloc_sbuf_tensor_at("a_lo", [P, BS, SB], F32R, offset=ring_at + 2 * BS * SB * 4)
        y_parts = nc.alloc_sbuf_tensor_at("y_parts", [P, 2, 2, HB, D], F32R, offset=ystage_at)
        z_rows = part[:, 0, :].rearrange("p (b d) -> p b d", d=D)
        z_hi = nc.alloc_sbuf_tensor_at("z_hi", [P, N], F32R, offset=ring_at)
        z_lo = nc.alloc_sbuf_tensor_at("z_lo", [P, N], F32R, offset=U_at)
        zst = nc.alloc_sbuf_tensor_at("zst", [P, 2, 2, P], F32R, offset=rsum_at)
        odd = ystage2.rearrange("p a h b d -> p (a h) (b d)")
        rows = [ring[:, 2, 4 * q:4 * q + 4, :].rearrange("p b i -> p (b i)") for q in range(2)]
        zi = ztmp[:, 0:2 * D].rearrange("p (q d) -> p q d", q=2)
        zg = [part[:, 1, :], diag.rearrange("p b i -> p (b i)")]
        zg = [v.rearrange("p (c d) -> p c d", d=D) for v in zg]
        cand, best8 = [stat[:, 0, :], stat[:, 1, :]], stat[:, 2, :]
        slot8 = stat[:, 3, :].bitcast(U32)
        topv = part[:, 0, 0:NB * TOPK].rearrange("p (b k) -> p b k", k=TOPK)
        S = part[:, 0, NB * TOPK:2 * NB * TOPK].rearrange("p (b k) -> p b k", k=TOPK)
        topi = part[:, 0, 2 * NB * TOPK:3 * NB * TOPK].bitcast(U32).rearrange("p (b k) -> p b k", k=TOPK)
        pairs = part[:, 0, 3 * NB * TOPK:4 * NB * TOPK].bitcast(U32).rearrange("p (b k) -> p b k", k=TOPK)
        acc, xin, obuf, osq, gath = (U[:, t * SB:(t + 1) * SB] for t in (0, 3, 4, 5, 6))
        gsum = U[:, SB:3 * SB].rearrange("p (i b d) -> p i b d", i=2, d=D)
        xin, obuf, osq = (v.rearrange("p (b d) -> p b d", b=BS) for v in (xin, obuf, osq))
        G = gath.rearrange("p (q k d) -> p q k d", q=2, k=TOPK)

        ps = ctx.enter_context(nc.psum_tensor("ps", [P, 8, CH], F32))
        PROD, BC, SMALL = 0, 4, 6

        half_sem = [sem(f"half_sem{s}") for s in range(2 * RING)]
        half_loaded = sem("half_loaded")
        consts_in = sem("consts_in")
        xt_in = [sem(f"xt_in{q}") for q in range(2)]
        const_step = sem("const_step")
        neg_step = sem("neg_step")
        b2_done = sem("b2_done")
        b2_kept = sem("b2_kept")
        xts_ready = sem("xts_ready")
        proj_done = sem("proj_done")
        proj_kept = sem("proj_kept")
        xw2_stored = [sem(f"xw2_stored{q}") for q in range(2)]
        xw2_loaded = sem("xw2_loaded")
        staged = [sem(f"staged{h}") for h in range(2)]
        w_used = [sem(f"w_used{h}") for h in range(2)]
        quarter_sem = [sem(f"quarter_sem{k}") for k in range(4)]
        quarter_loaded = sem("quarter_loaded")
        hi_ready = sem("hi_ready")
        lo_ready = sem("lo_ready")
        lo_shared = sem("lo_shared")
        y_lo_ready = [sem(f"y_lo_ready{h}") for h in range(2)]
        parts_used = sem("parts_used")
        sum_done = sem("sum_done")
        sum_kept = sem("sum_kept")
        part_done = sem("part_done")
        row_step = sem("row_step")
        rnat_done = sem("rnat_done")
        rn_copied = sem("rn_copied")
        d_ready = sem("d_ready")
        diag_staged = sem("diag_staged")
        y_ready = sem("y_ready")
        diag_ready = sem("diag_ready")
        bc_done = sem("bc_done")
        z_step = sem("z_step")
        zsq_ready = sem("zsq_ready")
        sq_done = sem("sq_done")
        zt_done = sem("zt_done")
        zt_kept = sem("zt_kept")
        z_stored = sem("z_stored")
        z_hi_ready = sem("z_hi_ready")
        z_lo_ready = sem("z_lo_ready")
        folded = sem("folded")
        pair_ready = sem("pair_ready")
        zi_sem = [sem(f"zi_sem{q}") for q in range(2)]
        zg_sem = [sem(f"zg_sem{q}") for q in range(2)]
        diff_done = sem("diff_done")
        diff_squared = sem("diff_squared")
        f_step = sem("f_step")
        odd_ready = sem("odd_ready")
        map_step = sem("map_step")
        split_step = sem("split_step")
        z_staged = sem("z_staged")
        scores_done = sem("scores_done")
        max_done = sem("max_done")
        row_free = sem("row_free")
        dist_step = sem("dist_step")
        root_done = sem("root_done")
        s_ready = sem("s_ready")
        deg_step = sem("deg_step")
        q_ready = sem("q_ready")
        q_stored = sem("q_stored")
        gidx_ready = sem("gidx_ready")
        g_sem = [sem(f"g_sem{q}") for q in range(2)]
        g_step = sem("g_step")
        turned = sem("turned")
        x_loaded = sem("x_loaded")
        ln_step = sem("ln_step")
        rstd_ready = sem("rstd_ready")
        out_stored = sem("out_stored")
        passed = sem("passed")

        Z_OPS, SPLIT_OPS, F_OPS, LN_OPS = 8, 5, 5, 11
        SHARE = 1
        PARTS = 2 * NS - 1

        def products_before(n):
            if n >= TILES_A:
                return QB + n - TILES_A
            i, r = divmod(n, NS)
            return i * (i + 1) // 2 + max(0, r - (NS - 1 - i))

        def over(column, n):
            return column.rearrange("p (b a) -> p b a", a=1).to_broadcast([P, BS, n])

        def plain(engine):
            engine.sem_inc(passed, 1)

        x_rows = x.rearrange("(i b p) d -> i p b d", b=BS, p=P)
        out_rows = out.rearrange("(i b p) d -> i p b d", b=BS, p=P)

        block = ctx.enter_context(nc.Block())

        @block.sync
        def _(sp):
            for dst, src in ((w12s[:, :], w12), (b1s[:, :], b1), (b2r, b2)):
                sp.dma_start(dst, src).then_inc(consts_in, 16)
            for q in range(2):
                cols = slice(q * N // 2, (q + 1) * N // 2)
                sp.dma_start(xt_all[:, cols], xt[:, cols]).then_inc(xt_in[q], 16)

            def pass_on(slot, h, turn):
                sp.wait_ge(half_sem[2 * slot + h], turn * 16 + 16)
                sp.sem_inc(half_loaded, 1)

            def load(slot, h, tile):
                sp.dma_start(ring[:, slot, h * HB:(h + 1) * HB, :],
                             at[tile, :, h * HB:(h + 1) * HB, :]).then_inc(half_sem[2 * slot + h], 16)

            tiles = [(i, r) for i in range(NS) for r in range(NS)]
            for n, (i, r) in enumerate(tiles):
                for h in range(2):
                    if n:
                        pass_on((n - 1) % RING, h, (n - 1) // RING)
                    if n >= RING:
                        sp.wait_ge(part_done, min(2 * (n - RING) + h + 1, 2 * TILES_A))
                        if products_before(n - RING + 1):
                            sp.wait_ge(w_used[h], products_before(n - RING + 1))
                    load(n % RING, h, i * NS + r)
            for h in range(2):
                pass_on((TILES_A - 1) % RING, h, (TILES_A - 1) // RING)

            def pass_quarter(k, turn):
                sp.wait_ge(quarter_sem[k], turn * 16 + 16)
                sp.sem_inc(quarter_loaded, 1)

            def load_tile(u, tile, fresh=False):
                for k in range(4):
                    if not (fresh and k < 2):
                        pass_quarter((k - 2) % 4, u + (-1 if k < 2 else 0))
                    if isinstance(u, int) and u == 0:
                        sp.wait_ge(part_done, 2 * TILES_A - 4)
                        sp.wait_ge(w_used[1], products_before(TILES_A - 2))
                    else:
                        sp.wait_ge(hi_ready, u * 4 + (k - 3))
                        sp.wait_ge(lo_ready, u * 4 + (k - 3))
                        if k == 3:
                            sp.wait_ge(lo_shared, u)
                    sp.dma_start(raw[:, 2 * k:2 * k + 2, :], at[tile, :, 2 * k:2 * k + 2, :]).then_inc(quarter_sem[k], 16)

            load_tile(0, (NS - 2) * NS, True)
            for m in range(2, NS):
                u0 = m * (m - 1) // 2
                with sp.Fori(0, m) as r:
                    load_tile(r + u0, r + (NS - 1 - m) * NS)
            for k in (2, 3):
                pass_quarter(k, TILES_B - 1)

            for h in range(2):
                sp.wait_ge(staged[h], QC)
                sp.wait_ge(y_lo_ready[h], TILES_B)
                sp.wait_ge(xw2_stored[h], NB // HB // 2 * 16)
            sp.dma_start(Y.rearrange("p (s b) d -> p s (b d)", b=HB),
                         xw2_dram.rearrange("s p c -> p s c")).then_inc(xw2_loaded, 16)

            load_tile(TILES_B, 0, True)
            for k in (2, 3):
                pass_quarter(k, TILES_B)
            sp.wait_ge(z_stored, 16 * NS)
            sp.wait_ge(z_step, Z_OPS * NS)
            z_nodes = z_dram.rearrange("(b p) (t d) -> b (p t) d", p=HP, t=2)

            def load_zi(b, q):
                sp.dma_start(zi[:, q, :], z_nodes[bass.ds(b, 1), :, :].rearrange("a p d -> (a p) d")
                             ).then_inc(zi_sem[q], 16)

            for q in range(2):
                load_zi(q, q)
            with sp.Fori(1, NB // 2) as g:
                for q in range(2):
                    sp.wait_ge(diff_done, g * 2 + (q - 1))
                    load_zi(g * 2 + q, q)

            load_tile(TILES_B + 1, 1, True)
            with sp.Fori(2, NS * NS) as c:
                load_tile(c + TILES_B, c)
            for k in (2, 3):
                pass_quarter(k, TILES_B + NS * NS - 1)

        @block.tensor
        def _(pe):
            def open_sums(row):
                if not (isinstance(row, int) and row < 2):
                    pe.wait_ge(sum_kept, row - 1)
                for c in range(2):
                    pe.matmul(ps[:, (row % 2) * 2 + c, :], zeros[:, 0:P], zeros[:, :], start=True, stop=False,
                              skip_group_check=True)

            def product(q, n, row, close=False):
                for c in range(2):
                    for b in range(BS):
                        if c == 0 and b % HB == 0:
                            pe.wait_ge(half_loaded, n * 2 + (1 + b // HB))
                            pe.wait_ge(staged[b // HB], q + 1)
                        mm = pe.matmul(ps[:, (row % 2) * 2 + c, :], ystage[:, b // HB, b % HB, :],
                                       ring[:, n % RING, b, c * CH:(c + 1) * CH],
                                       start=False, stop=(b == BS - 1), skip_group_check=True)
                        if c == 1 and b % HB == HB - 1:
                            mm.then_inc(w_used[b // HB], 1)

            def product_of_parts(q, row):
                u = q - QB if isinstance(q, int) else q + (-QB)
                for k in range(4):
                    h = k // 2
                    pe.wait_ge(hi_ready, u * 4 + (k + 1))
                    pe.wait_ge(lo_ready, u * 4 + (k + 1))
                    if k == 3:
                        pe.wait_ge(lo_shared, u + 1)
                    if k % 2 == 0:
                        pe.wait_ge(staged[h], q + 1)
                        pe.wait_ge(y_lo_ready[h], u + 1)
                    for c in range(2):
                        for b in (2 * k, 2 * k + 1):
                            for y, a in ((0, a_hi), (0, a_lo), (1, a_hi)):
                                mm = pe.matmul(ps[:, (row % 2) * 2 + c, :], y_parts[:, h, y, b % HB, :],
                                               a[:, b, c * CH:(c + 1) * CH],
                                               start=False, stop=(k == 3 and b == BS - 1 and y == 1),
                                               skip_group_check=True)
                    mm.then_inc(parts_used, 1)

            def close_sums(q, of_parts=True):
                if not of_parts:
                    pe.wait_ge(w_used[1], q + 1)
                else:
                    pe.wait_ge(parts_used, (q + (1 - QB)) * 4)
                pe.sem_inc(sum_done, 1)

            def spread_d(f):
                pe.wait_ge(diag_ready, f + 1)
                if f:
                    pe.wait_ge(split_step, SPLIT_OPS * f)
                for c in range(2):
                    mm = pe.matmul(ps[:, BC + c, :], ones[:, :],
                                   diag[:, c * HB:(c + 1) * HB, :].rearrange("p b i -> p (b i)"),
                                   start=True, stop=True)
                mm.then_inc(bc_done, 1)

            def squares(f):
                pe.wait_ge(zsq_ready, f + 1)
                for c in range(2):
                    mm = pe.matmul(ps[:, BC + c, :], ones[:, :], zsq[:, c * CH:(c + 1) * CH], start=True, stop=True)
                mm.then_inc(sq_done, 1)
                if f:
                    pe.wait_ge(zt_kept, f)
                for b in range(BS):
                    mm = pe.transpose(ps[:, SMALL + b // HB, (b % HB) * P:(b % HB + 1) * P],
                                      U[:, ((NS - 1 - f) * BS + b) * P:((NS - 1 - f) * BS + b + 1) * P], ident[:, :])
                mm.then_inc(zt_done, 1)

            pe.wait_ge(const_step, 5)
            pe.wait_ge(consts_in, 48)
            pe.matmul(ps[:, SMALL, 0:D], ones[0:1, :], b2r, start=True, stop=True).then_inc(b2_done, 1)
            with pe.Fori(0, NB // HB // 2) as g:
                for q in range(2):
                    pe.wait_ge(xts_ready, g * 2 + (q + 1))
                    pe.wait_ge(proj_kept, g * 4 + 2 * q)
                    for b in range(HB):
                        mm = pe.matmul(ps[:, 2 * q + b // 2, (b % 2) * 2 * D:(b % 2 + 1) * 2 * D],
                                       xts[:, q, b * P:(b + 1) * P], w12s[:, :], start=True, stop=True)
                    mm.then_inc(proj_done, 1)
            pe.wait_ge(proj_kept, 2 * NB // HB)
            pe.wait_ge(b2_kept, 1)
            for i in range(NS):
                q0 = i * (i + 1) // 2
                open_sums(i)
                if i:
                    with pe.Fori(0, i) as k:
                        product(k + q0, k + (NS * i + NS - 1 - i), i)
                pe.wait_ge(row_step, PARTS * (i + 1))
                if i:
                    pe.wait_ge(rn_copied, i)
                pe.matmul(ps[:, SMALL, 0:BS], zeros[:, 0:P], zeros[:, 0:BS], start=True, stop=False,
                          skip_group_check=True)
                for v in (rsum[:, :], part[:, 1, :]):
                    for b in range(BS):
                        mm = pe.matmul(ps[:, SMALL, b:b + 1], v[:, b * P:(b + 1) * P], ones[:, 0:1],
                                       start=False, stop=True, skip_group_check=True)
                    pe.wait_ge(part_done, 2 * NS * (i + 1))
                mm.then_inc(rnat_done, 1)
                product(q0 + i, NS * i + NS - 1, i)
                close_sums(q0 + i, False)
            spread_d(0)
            pe.wait_ge(rn_copied, NS)
            for m in range(1, NS):
                q0 = QB + m * (m - 1) // 2
                row = NS - 1 + m
                open_sums(row)
                for k in range(min(m, 3)):
                    product_of_parts(q0 + k, row)
                squares(m - 1)
                if m > 3:
                    with pe.Fori(3, m) as k:
                        product_of_parts(k + q0, row)
                close_sums(q0 + m - 1)
                spread_d(m)
            squares(NS - 1)

            pe.wait_ge(split_step, SPLIT_OPS * NS)
            with pe.Fori(0, NB // 4) as g:
                for q in range(4):
                    pe.wait_ge(z_staged, g * 8 + (2 * q + 2))
                    for cc in range(NS):
                        pair = 2 * (cc % 4)
                        pe.wait_ge(z_lo_ready, cc + 1)
                        pe.wait_ge(folded, g * (4 * NS) + (NS * q + cc + 1))
                        for c in range(2):
                            cols = slice((2 * cc + c) * CH, (2 * cc + c + 1) * CH)
                            for t, (w, v) in enumerate(((0, z_hi), (0, z_lo), (1, z_hi))):
                                pe.matmul(ps[:, pair + c, :], zst[:, q % 2, w, :], v[:, cols],
                                          start=(t == 0), stop=False)
                            mm = pe.matmul(ps[:, pair + c, :], negsel[:, :], sqp[:, cols], start=False, stop=True)
                        mm.then_inc(scores_done, 1)

            def turn(i):
                pe.wait_ge(sum_kept, i + (2 * NS))
                pe.wait_ge(ln_step, i * LN_OPS)
                for b in range(BS):
                    mm = pe.transpose(ps[:, BC + b // HB, (b % HB) * P:(b % HB + 1) * P],
                                      acc[:, b * P:(b + 1) * P], ident[:, :])
                mm.then_inc(turned, 1)

            pe.wait_ge(folded, 4 + NS * NB)

            def row_c(i, later):
                row = i + (2 * NS - 1)
                open_sums(row)
                product_of_parts(i * NS + QC, row)
                if later:
                    turn(i - 1)
                with pe.Fori(1, NS) as r:
                    product_of_parts(i * NS + r + QC, row)
                close_sums(i * NS + (QC + NS - 1))

            row_c(0, False)
            with pe.Fori(1, NS) as i:
                row_c(i, True)
            turn(NS - 1)

        @block.scalar
        def _(act):
            def stage(q, j):
                for h in range(2):
                    if not (isinstance(q, int) and q == 0):
                        act.wait_ge(w_used[h], q)
                    act.activation(ystage[:, h, :, :], Y[:, bass.ds(j * BS + h * HB, HB), :],
                                   ACT.Copy).then_inc(staged[h], 1)

            def stage_scaled(q, j):
                act.wait_ge(d_ready, j + 1)
                for h in range(2):
                    if q:
                        act.wait_ge(w_used[h], q)
                    for b in range(HB):
                        blk = j * BS + h * HB + b
                        ins = act.activation(ystage[:, h, b, :], Y[:, blk, :], ACT.Copy, scale=dn[:, blk:blk + 1])
                    ins.then_inc(staged[h], 1)
                act.wait_ge(staged[1], q + 1)
                act.sem_inc(diag_staged, 1)

            def first_of_weights(q, j, h):
                act.activation(y_parts[:, h, 0, :, :], Y[:, bass.ds(j * BS + h * HB, HB), :],
                               ACT.Copy).then_inc(staged[h], 1)

            def first_of_tile(u, k):
                act.wait_ge(quarter_loaded, u * 4 + (k + 1))
                if not (isinstance(u, int) and u == 0):
                    act.wait_ge(parts_used, u * 4 + (k - 3))
                act.activation(a_hi[:, 2 * k:2 * k + 2, :], raw[:, 2 * k:2 * k + 2, :],
                               ACT.Copy).then_inc(hi_ready, 1)

            def first_parts(q, j, between=None):
                u = q - QB if isinstance(q, int) else q + (-QB)
                for h in range(2):
                    if isinstance(u, int) and u == 0:
                        act.wait_ge(w_used[h], q)
                    else:
                        act.wait_ge(parts_used, u * 4 + (2 * h - 2))
                    first_of_weights(q, j, h)
                    for k in (2 * h, 2 * h + 1):
                        first_of_tile(u, k)
                    if h == 0 and between:
                        between()

            act.wait_ge(b2_done, 1)
            act.activation(b2b[:, 0, :], ps[:, SMALL, 0:D], ACT.Copy).then_inc(b2_kept, 1)

            def feed_xt(s, q):
                act.activation(xts[:, q, :], xt_all[:, bass.ds(s * CH, CH)], ACT.Copy).then_inc(xts_ready, 1)

            for q in range(2):
                act.wait_ge(xt_in[q], 16)
            for q in range(2):
                feed_xt(q, q)
            with act.Fori(0, NB // HB // 2) as g:
                for q in range(2):
                    both = ps[:, 2 * q:2 * q + 2, :].rearrange("p c (b w d) -> p (c b) w d", w=2, d=D)
                    act.wait_ge(proj_done, g * 2 + (q + 1))
                    act.activation(Y[:, bass.ds((g * 2 + q) * HB, HB), :], both[:, :, 0, :],
                                   ACT.Copy).then_inc(proj_kept, 1)
                    act.wait_ge(xw2_stored[q], g * 16)
                    act.activation(xw2s[:, q, :].rearrange("p (b d) -> p b d", d=D), both[:, :, 1, :],
                                   ACT.Copy).then_inc(proj_kept, 1)
                    feed_xt((g * 2 + (q + 2)) % (NB // HB), q)
                    act.wait_ge(proj_kept, g * 4 + (2 * q + 2))
                    act.dma_start(xw2_dram[bass.ds(g * 2 + q, 1), :, :].rearrange("s p c -> (s p) c"),
                                  xw2s[:, q, :]).then_inc(xw2_stored[q], 16)

            act.wait_ge(xts_ready, NB // HB + 2)
            for i in range(NS):
                q0 = i * (i + 1) // 2
                if i > 1:
                    with act.Fori(1, i) as k:
                        stage(k + q0, k)
                act.wait_ge(rnat_done, i + 1)
                act.activation(rn[:, i * BS:(i + 1) * BS], ps[:, SMALL, 0:BS], ACT.Copy).then_inc(rn_copied, 1)
                stage_scaled(q0 + i, i)
                act.wait_ge(y_ready, i + 1)
                if i < NS - 1:
                    stage(q0 + i + 1, 0)
                act.wait_ge(sum_done, i + 1)
                act.activation(U[:, i * SB:(i + 1) * SB].rearrange("p (c i) -> p c i", c=2),
                               ps[:, 2 * (i % 2):2 * (i % 2) + 2, :], ACT.Copy).then_inc(sum_kept, 1)

            def square(f):
                act.wait_ge(z_step, Z_OPS * (f + 1))
                if f:
                    act.wait_ge(sq_done, f)
                act.activation(zsq, U[:, (NS - 1 - f) * SB:(NS - f) * SB],
                               ACT.Square).then_inc(zsq_ready, 1)

            def store_z(f):
                act.wait_ge(zt_done, f + 1)
                if f:
                    act.wait_ge(z_stored, 16 * f)
                act.activation(z_rows.rearrange("p b d -> p (b d)"),
                               ps[:, SMALL:SMALL + 2, :].rearrange("p c i -> p (c i)"), ACT.Copy).then_inc(zt_kept, 1)
                act.wait_ge(zt_kept, f + 1)
                act.dma_start(z_dram[(NS - 1 - f) * HSB:(NS - f) * HSB, :].rearrange(
                    "(b p) (t d) -> (p t) b d", p=HP, t=2), z_rows).then_inc(z_stored, 16)

            for m in range(1, NS):
                q0 = QB + m * (m - 1) // 2
                for k in range(min(m, 3)):
                    first_parts(q0 + k, NS - m + k, (lambda: square(m - 1)) if k == 2 else None)
                if m < 3:
                    square(m - 1)
                if m > 3:
                    with act.Fori(3, m) as k:
                        first_parts(k + q0, k + (NS - m))
                store_z(m - 1)
            square(NS - 1)
            store_z(NS - 1)

            act.wait_ge(sum_kept, 2 * NS - 1)
            act.wait_ge(parts_used, 4 * TILES_B)
            for j in range(NS):
                act.activation(z_hi[:, j * SB:(j + 1) * SB], U[:, j * SB:(j + 1) * SB], ACT.Copy
                               ).then_inc(z_hi_ready, 1)

            def keep_odd(b, cc):
                act.wait_ge(scores_done, b * NS + (cc + 1))
                act.wait_ge(folded, b * NS + (cc + 1))
                act.activation(odd[:, cc % 4, :], ps[:, 2 * (cc % 4):2 * (cc % 4) + 2, :].rearrange(
                    "p c (n t) -> p (c n) t", t=2)[:, :, 1], ACT.Copy).then_inc(odd_ready, 1)

            def square_diff(b, q):
                act.wait_ge(diff_done, b + 1)
                for c in range(2 * TOPK):
                    ins = act.activation(zg[q][:, c, :], zg[q][:, c, :], ACT.Square, accum_out=cand[q][:, c:c + 1])
                ins.then_inc(diff_squared, 1)

            for b in range(2):
                for cc in range(NS):
                    keep_odd(b, cc)
            with act.Fori(1, NB // 2) as g:
                for q in range(2):
                    for cc in range(NS):
                        keep_odd(g * 2 + q, cc)
                        if cc == 5:
                            square_diff(g * 2 + (q - 2), q)
            act.wait_ge(scores_done, NB * NS)
            act.wait_ge(z_staged, 2 * NB)
            for k in range(4):
                first_of_tile(TILES_B, k)
            for q in range(2):
                square_diff(NB - 2 + q, q)

            act.wait_ge(dist_step, 1)
            act.activation(S, topv, ACT.Sqrt).then_inc(root_done, 1)
            act.wait_ge(root_done, 1)
            act.activation(S, S, ACT.Exp, scale=-0.5).then_inc(s_ready, 1)

            act.wait_ge(deg_step, 2)
            act.activation(d2n[:, :], d2n[:, :], ACT.Sqrt).then_inc(root_done, 1)

            def keep_sums(i):
                act.wait_ge(sum_done, i + (2 * NS))
                act.wait_ge(turned, i)
                act.activation(acc.rearrange("p (c i) -> p c i", c=2),
                               ps[:, bass.ds(((i + 1) % 2) * 2, 2), :], ACT.Copy).then_inc(sum_kept, 1)

            act.wait_ge(q_ready, 1)
            for h in range(2):
                act.wait_ge(parts_used, 4 * TILES_B)
                first_of_weights(QC, 1, h)
            with act.Fori(1, NS) as r:
                act.wait_ge(q_ready, r + 1)
                first_parts(r + QC, (r + 1) % NS)
            with act.Fori(1, NS) as i:
                first_parts(i * NS + QC, (i + 1) % NS)
                keep_sums(i - 1)
                with act.Fori(1, NS) as r:
                    first_parts(i * NS + r + QC, (i + 1 + r) % NS)
            keep_sums(NS - 1)

        @block.vector
        def _(dve):
            def sum_half(n, h):
                dve.wait_ge(half_loaded, n * 2 + (h + 1))
                dve.tensor_reduce(part[:, h, :],
                                  ring[:, n % RING, h * HB:(h + 1) * HB, :].rearrange("p b i -> p i b"),
                                  AX.X, ALU.add).then_inc(part_done, 1)

            with dve.Fori(0, NS) as i:
                dve.wait_ge(row_step, i * PARTS)
                sum_half(i * NS, 0)
                dve.wait_ge(rnat_done, i)
                sum_half(i * NS, 1)
                with dve.Fori(0, NS - 1) as r:
                    for h in range(2):
                        dve.wait_ge(row_step, i * PARTS + r * 2 + (h + 1))
                        sum_half(i * NS + r + 1, h)

            dve.wait_ge(rnat_done, NS)
            dve.wait_ge(b2_done, 1)

            def second_part(u, k):
                blocks = slice(2 * k, min(2 * k + 2, BS - SHARE))
                dve.wait_ge(hi_ready, u * 4 + (k + 1))
                dve.tensor_tensor(a_lo[:, blocks, :], raw[:, blocks, :], a_hi[:, blocks, :].bitcast(F32),
                                  ALU.subtract).then_inc(lo_ready, 1)

            def second_parts(u):
                for k in range(4):
                    second_part(u, k)

            def finish(f, c, fresh):
                sup = (f * (NS - 1) + (NS - 1)) % NS

                def z_op(k, instruction):
                    instruction.then_inc(z_step, 1)
                    dve.wait_ge(z_step, f * Z_OPS + (k + 1))

                dve.wait_ge(bc_done, f + 1)
                dve.wait_ge(sum_kept, NS)
                u = U[:, bass.ds(sup * SB + c * CH, CH)]
                if fresh:
                    z_op(4 * c, dve.tensor_copy(ztmp[:, :], u))
                else:
                    dve.wait_ge(sum_done, f + NS)
                    z_op(4 * c, dve.tensor_tensor(ztmp[:, :], u, ps[:, ((f + 1) % 2) * 2 + c, :], ALU.add))
                    if c == 1:
                        dve.sem_inc(sum_kept, 1)
                z_op(4 * c + 1, dve.tensor_tensor(ztmp[:, :], ztmp[:, :], ps[:, BC + c, :], ALU.mult))
                z_op(4 * c + 2, dve.tensor_scalar(ztmp[:, :], ztmp[:, :], b1s[:, :], None, ALU.add))
                z_op(4 * c + 3, dve.scalar_tensor_tensor(out=u, in0=ztmp[:, :], scalar=0.1, in1=ztmp[:, :],
                                                         op0=ALU.mult, op1=ALU.max))

            def split(f):
                sup = (f * (NS - 1) + (NS - 1)) % NS
                dve.wait_ge(sq_done, f + 1)
                sq = ps[:, BC:BC + 2, :].rearrange("p c i -> p (c i)")
                cols = bass.ds(sup * SB, SB)
                dve.tensor_copy(sqp[:, cols], sq).then_inc(split_step, 1)
                for t, p0 in enumerate((64, 96)):
                    dve.wait_ge(split_step, f * SPLIT_OPS + (2 * t + 1))
                    dve.tensor_tensor(resid[p0:P, :], sq[p0:P, :] if t == 0 else resid[p0:P, :],
                                      sqp[p0:P, cols], ALU.subtract).then_inc(split_step, 1)
                    dve.wait_ge(split_step, f * SPLIT_OPS + (2 * t + 2))
                    plain(dve)
                    dve.tensor_copy(sqp[p0:P, cols], resid[p0:P, :]).then_inc(split_step, 1)

            for m in range(1, NS):
                u0 = m * (m - 1) // 2
                for r in range(min(m, 4)):
                    second_parts(u0 + r)
                    for c in range(2):
                        if r == min(c, m - 1):
                            finish(m - 1, c, m == 1)
                    if r == 3:
                        split(m - 1)
                if m < 4:
                    split(m - 1)
                if m > 4:
                    with dve.Fori(4, m) as r:
                        second_parts(r + u0)
            for c in range(2):
                finish(NS - 1, c, False)
            split(NS - 1)

            dve.wait_ge(zt_done, NS)
            for j in range(NS):
                dve.wait_ge(z_hi_ready, j + 1)
                cols = slice(j * SB, (j + 1) * SB)
                dve.tensor_tensor(z_lo[:, cols], U[:, cols], z_hi[:, cols].bitcast(F32), ALU.subtract
                                  ).then_inc(z_lo_ready, 1)
            dve.wait_ge(sq_done, NS)
            dve.wait_ge(parts_used, 4 * TILES_B)
            dve.wait_ge(z_stored, 16 * NS)
            dve.sem_inc(row_free, 2)
            dve.wait_ge(split_step, SPLIT_OPS * NS)
            dve.wait_ge(zt_kept, NS)
            dve.sem_inc(folded, 4)

            def fold(b, q, chunks):
                for cc in chunks:
                    dve.wait_ge(odd_ready, b * NS + (cc + 1))
                    if cc == 0:
                        dve.wait_ge(row_free, b + 1)
                    even = ps[:, 2 * (cc % 4):2 * (cc % 4) + 2, :].rearrange("p c (n t) -> p (c n) t", t=2)[:, :, 0]
                    dve.tensor_tensor(rows[q][:, cc * CH:(cc + 1) * CH], even, odd[:, cc % 4, :], ALU.max
                                      ).then_inc(folded, 1)

            def best(b, q):
                dve.wait_ge(folded, b * NS + (NS + 4))
                plain(dve)
                dve.max(top8[:, q, :], rows[q]).then_inc(max_done, 1)

            def find(b, q):
                dve.wait_ge(max_done, b + 1)
                plain(dve)
                dve.max_index(idx8[:, q, :], top8[:, q, :], rows[q]).then_inc(row_free, 1)

            def keep_pairs(b, q):
                dve.wait_ge(row_free, b + 3)
                plain(dve)
                dve.tensor_copy(pairs[:, bass.ds(b, 1), :], idx8[:, q:q + 1, 0:TOPK]).then_inc(pair_ready, 1)
                dve.tensor_copy(gidx[:, q, :], idx8[:, q, 0:TOPK]).then_inc(pair_ready, 1)

            def negate(b, q):
                dve.wait_ge(diff_squared, b + 1)
                dve.tensor_scalar(ncand[:, :], cand[q], -1.0, None, ALU.mult).then_inc(f_step, 1)

            def order(b):
                dve.wait_ge(f_step, b * F_OPS + 1)
                plain(dve)
                dve.max(best8, ncand[:, :]).then_inc(f_step, 1)

            def place(b):
                dve.wait_ge(f_step, b * F_OPS + 2)
                plain(dve)
                dve.max_index(slot8, best8, ncand[:, :]).then_inc(f_step, 1)

            def keep_nearest(b):
                dve.wait_ge(f_step, b * F_OPS + 3)
                plain(dve)
                dve.tensor_copy(topv[:, bass.ds(b, 1), :], stat[:, 2:3, 0:TOPK]).then_inc(f_step, 1)
                dve.tensor_copy(topi[:, bass.ds(b, 1), :], stat[:, 3:4, 0:TOPK].bitcast(U32)).then_inc(f_step, 1)
                dve.wait_ge(f_step, b * F_OPS + 5)

            def decide(b, q):
                negate(b, q)
                order(b)
                place(b)
                keep_nearest(b)

            def search(b, q):
                fold(b, q, (0,))
                best(b - 1, 1 - q)
                fold(b, q, (1, 2, 3, 4))
                find(b - 1, 1 - q)
                fold(b, q, (5,))
                negate(b - 2, q)
                keep_pairs(b - 1, 1 - q)
                order(b - 2)
                fold(b, q, (6,))
                place(b - 2)
                fold(b, q, (7,))
                keep_nearest(b - 2)

            fold(0, 0, range(NS))
            fold(1, 1, (0, 1))
            best(0, 0)
            fold(1, 1, (2, 3, 4))
            find(0, 0)
            keep_pairs(0, 0)
            fold(1, 1, (5, 6, 7))
            for q in range(2):
                search(2 + q, q)
            with dve.Fori(1, NB // 4) as g:
                for q in range(4):
                    search(g * 4 + q, q % 2)
            best(NB - 1, 1)
            find(NB - 1, 1)
            keep_pairs(NB - 1, 1)
            decide(NB - 2, 0)
            dve.wait_ge(row_free, NB + 2)
            second_parts(TILES_B)
            decide(NB - 1, 1)

            dve.tensor_scalar(topv, topv, -1.0, EPS_D2, ALU.mult, ALU.add).then_inc(dist_step, 1)
            flat = diag.rearrange("p b i -> p (b i)")
            c_f, p_f, w_step, term = (flat[:, t * NB * TOPK:(t + 1) * NB * TOPK].rearrange("p (b k) -> p b k", k=TOPK)
                                      for t in range(4))
            node = ztmp[:, 0:NB * TOPK].rearrange("p (b k) -> p b k", k=TOPK)
            maps = [0]

            def mapped(instruction):
                instruction.then_inc(map_step, 1)
                maps[0] += 1
                dve.wait_ge(map_step, maps[0])

            def node_step(k):
                mapped(dve.tensor_scalar(term, c_f, 2.0 * k, None, ALU.is_ge))
                mapped(dve.tensor_tensor(term, term, w_step[:, :, k:k + 1].to_broadcast([P, NB, TOPK]), ALU.mult))
                mapped(dve.tensor_tensor(node, node, term, ALU.add))

            mapped(dve.tensor_copy(c_f, topi))
            mapped(dve.tensor_copy(p_f, pairs))
            mapped(dve.tensor_tensor(w_step[:, :, 1:TOPK], p_f[:, :, 1:TOPK], p_f[:, :, 0:TOPK - 1], ALU.subtract))
            mapped(dve.tensor_scalar(w_step[:, :, 1:TOPK], w_step[:, :, 1:TOPK], 2.0, -2.0, ALU.mult, ALU.add))
            mapped(dve.tensor_scalar(term, p_f[:, :, 0:1].to_broadcast([P, NB, TOPK]), 2.0, None, ALU.mult))
            mapped(dve.tensor_tensor(node, term, c_f, ALU.add))
            node_step(1)
            dve.wait_ge(s_ready, 1)
            dve.tensor_reduce(d2n[:, :], S, AX.X, ALU.add).then_inc(deg_step, 1)
            dve.wait_ge(deg_step, 1)
            dve.tensor_tensor(d2n[:, :], d2n[:, :], rn[:, :], ALU.add).then_inc(deg_step, 1)
            node_step(2)
            dve.wait_ge(root_done, 2)
            dve.reciprocal(d2n[:, :], d2n[:, :]).then_inc(deg_step, 1)
            dve.wait_ge(deg_step, 3)
            dve.wait_ge(xw2_loaded, 16)
            for j in [*range(1, NS), 0]:
                yj = Y[:, j * BS:(j + 1) * BS, :]
                dve.tensor_tensor(yj, yj, over(d2n[:, j * BS:(j + 1) * BS], D), ALU.mult).then_inc(q_ready, 1)

            node_step(3)
            mapped(dve.tensor_copy(topi, node))

            dve.tensor_copy(gidx[:, 0, :], topi[:, 0, :]).then_inc(gidx_ready, 1)

            def weighted_sum(row, col, blk, t, n):
                dve.wait_ge(g_sem[t], n * (16 * TOPK))
                gs = gsum[:, row % 2, bass.ds(col, 1), :].rearrange("p a d -> p (a d)")
                for k in range(TOPK):
                    sk = S[:, bass.ds(blk, 1), k:k + 1].rearrange("p a k -> p (a k)")
                    if k == 0:
                        dve.tensor_scalar(gs, G[:, t, k, :], sk, None, ALU.mult).then_inc(g_step, 1)
                    else:
                        dve.wait_ge(g_step, blk * TOPK + k)
                        dve.scalar_tensor_tensor(out=gs, in0=G[:, t, k, :], scalar=sk, in1=gs,
                                                 op0=ALU.mult, op1=ALU.add).then_inc(g_step, 1)

            def pair(i, rr, first=False, after_first=False, between=()):
                for t in range(2):
                    blk = i * BS + rr * 2 + t
                    if not first and not (after_first and t == 0):
                        second_parts(blk + TILES_B)
                    elif first and t == 1:
                        second_parts(blk + TILES_B)
                        second_parts(blk + (TILES_B + 1))
                    if t == 1:
                        weighted_sum(i, rr * 2, blk - 1, 0, i * HB + rr + 1)
                    elif isinstance(rr, int) and rr == 0:
                        if not first:
                            weighted_sum(i + 1, BS - 1, blk - 1, 1, i * HB)
                    else:
                        weighted_sum(i, rr * 2 - 1, blk - 1, 1, i * HB + rr)
                    if not (first and t == 0):
                        dve.wait_ge(g_step, blk * TOPK)
                    dve.tensor_copy(gidx[:, 1 - t:2 - t, :],
                                    topi[:, bass.ds((blk + 1) % NB, 1), :]).then_inc(gidx_ready, 1)
                    for step in between[t:t + 1]:
                        step(i - 1)

            def ln(i, steps):
                for n, step in steps:
                    if n:
                        dve.wait_ge(ln_step, i * LN_OPS + n)
                    step().then_inc(ln_step, 1)

            def residual(i):
                dve.wait_ge(turned, i + 1)
                ln(i, [(0, lambda: dve.tensor_tensor(obuf.rearrange("p b d -> p (b d)"),
                                                     ps[:, BC:BC + 2, :].rearrange("p c i -> p (c i)"),
                                                     gsum[:, i % 2, :, :].rearrange("p b d -> p (b d)"), ALU.add)),
                       (1, lambda: dve.tensor_tensor(obuf, obuf, over(d2n[:, bass.ds(i * BS, BS)], D), ALU.mult))])

            def add_x(i):
                dve.wait_ge(x_loaded, (i + 1) * 16)
                ln(i, [(2, lambda: dve.tensor_tensor(xin, xin, b2b[:, :, :].to_broadcast([P, BS, D]), ALU.add)),
                       (3, lambda: dve.tensor_tensor(obuf, obuf, xin, ALU.add))])

            def centre(i):
                ln(i, [(4, lambda: dve.tensor_reduce(stat[:, 0, :], obuf, AX.X, ALU.add)),
                       (5, lambda: dve.tensor_scalar(stat[:, 1, :], stat[:, 0, :], 1.0 / D, None, ALU.mult)),
                       (6, lambda: dve.tensor_tensor(obuf, obuf, over(stat[:, 1, :], D), ALU.subtract))])

            def variance(i):
                dve.wait_ge(out_stored, i * 16)
                ln(i, [(7, lambda: dve.tensor_tensor(osq, obuf, obuf, ALU.mult)),
                       (8, lambda: dve.tensor_reduce(stat[:, 2, :], osq, AX.X, ALU.add)),
                       (9, lambda: dve.tensor_scalar(stat[:, 3, :], stat[:, 2, :], 1.0 / D, EPS_LN,
                                                     ALU.mult, ALU.add))])

            def scale_row(i):
                dve.wait_ge(rstd_ready, i + 1)
                dve.wait_ge(ln_step, i * LN_OPS + (LN_OPS - 1))
                dve.tensor_tensor(osq, obuf, over(stat[:, 3, :], D), ALU.mult).then_inc(ln_step, 1)

            pair(0, 0, True)
            pair(0, 1, after_first=True)
            with dve.Fori(2, HB) as rr:
                pair(0, rr)
            with dve.Fori(1, NS) as i:
                pair(i, 0, between=(lambda _: None, residual))
                pair(i, 1, between=(add_x, centre))
                pair(i, 2, between=(variance,))
                pair(i, 3, between=(scale_row,))
            weighted_sum(NS + 1, BS - 1, NB - 1, 1, NS * HB)
            dve.wait_ge(g_step, NB * TOPK)
            for step in (residual, add_x, centre, variance, scale_row):
                step(NS - 1)

        @block.gpsimd
        def _(pool):
            pool.memset(ident[:, :], 0.0).then_inc(const_step, 1)
            pool.memset(ones[:, :], 1.0).then_inc(const_step, 1)
            pool.memset(mhalf[:, :], -0.5).then_inc(const_step, 1)
            pool.memset(negsel[:, :], 0.0).then_inc(const_step, 1)
            pool.memset(zeros[:, :], 0.0).then_inc(const_step, 1)
            pool.wait_ge(const_step, 5)
            pool.affine_select(out=ident[:, :], in_=ident[:, :], compare_op=ALU.not_equal, fill=1.0, base=0,
                               pattern=[[-1, P]], channel_multiplier=1).then_inc(neg_step, 1)
            for t, p0 in enumerate((0, 64, 96)):
                pool.wait_ge(neg_step, t + 1)
                pool.memset(negsel[p0:p0 + 1, :], -1.0).then_inc(neg_step, 1)
            pool.wait_ge(neg_step, 4)

            def make_diag(f):
                if f:
                    pool.wait_ge(bc_done, f)
                j = NS - 1 - f
                pool.tensor_tensor(diag[:, :, :],
                                   ident[:, :].rearrange("p (a i) -> p a i", a=1).to_broadcast([P, BS, P]),
                                   over(dn[:, j * BS:(j + 1) * BS], P), ALU.mult).then_inc(diag_ready, 1)

            with pool.Fori(0, NS) as i:
                def add_part(done, s, fresh, h):
                    pool.wait_ge(part_done, done)
                    if fresh:
                        plain(pool)
                        pool.tensor_copy(rsum[:, :], part[:, h, :]).then_inc(row_step, 1)
                    else:
                        pool.wait_ge(row_step, s)
                        pool.tensor_tensor(rsum[:, :], rsum[:, :], part[:, h, :], ALU.add).then_inc(row_step, 1)

                pool.wait_ge(rnat_done, i)
                add_part(i * (2 * NS) + 1, i * PARTS, True, 0)
                with pool.Fori(0, NS - 1) as r:
                    add_part(i * (2 * NS) + r * 2 + 2, i * PARTS + r * 2 + 1, False, 1)
                    add_part(i * (2 * NS) + r * 2 + 3, i * PARTS + r * 2 + 2, False, 0)

                pool.wait_ge(rn_copied, i + 1)
                cols = bass.ds(i * BS, BS)
                pool.tensor_tensor(dn[:, cols], rn[:, cols], mhalf[:, 0:BS], ALU.pow).then_inc(d_ready, 1)
                pool.wait_ge(d_ready, i + 1)
                pool.wait_ge(diag_staged, i + 1)
                pool.tensor_tensor(Y[:, cols, :], Y[:, cols, :], over(dn[:, cols], D), ALU.mult).then_inc(y_ready, 1)

            pool.wait_ge(xw2_stored[0], NB // HB // 2 * 16)
            pool.wait_ge(xw2_stored[1], NB // HB // 2 * 16)

            def second_of_weights(q, j, h):
                pool.wait_ge(staged[h], q + 1)
                pool.tensor_tensor(y_parts[:, h, 1, :, :], Y[:, bass.ds(j * BS + h * HB, HB), :],
                                   y_parts[:, h, 0, :, :].bitcast(F32), ALU.subtract).then_inc(y_lo_ready[h], 1)

            def share_of_tile(u):
                pool.wait_ge(hi_ready, u * 4 + 4)
                blocks = slice(BS - SHARE, BS)
                pool.tensor_tensor(a_lo[:, blocks, :], raw[:, blocks, :], a_hi[:, blocks, :].bitcast(F32),
                                   ALU.subtract).then_inc(lo_shared, 1)

            def second_share(q, j, between=()):
                for h in range(2):
                    second_of_weights(q, j, h)
                    for gather_one in between[2 * h:2 * h + 2]:
                        gather_one()
                share_of_tile(q - QB if isinstance(q, int) else q + (-QB))

            make_diag(0)
            for m in range(1, NS):
                q0 = QB + m * (m - 1) // 2
                second_share(q0, NS - m)
                make_diag(m)
                if m > 1:
                    with pool.Fori(1, m) as k:
                        second_share(k + q0, k + (NS - m))

            pool.wait_ge(split_step, SPLIT_OPS * NS)

            def double(b, q):
                for t, v in enumerate((z_hi, z_lo)):
                    zb = v[:, bass.ds(b * P, P)].bitcast(F32)
                    pool.tensor_tensor(zst[:, q, t, :], zb, zb, ALU.add).then_inc(z_staged, 1)

            def gather_pairs(b, q, ks):
                for k in ks:
                    if k == 0:
                        pool.wait_ge(pair_ready, b * 2 + 2)
                        plain(pool)
                    pool.indirect_dma_start(zg[q][:, 2 * k:2 * k + 2, :].rearrange("p c d -> p (c d)"), None, z_dram,
                                            bass.IndirectOffsetOnAxis(ap=gidx[:, q, k:k + 1], axis=0)
                                            ).then_inc(zg_sem[q], 16)

            def difference(b, q, n):
                pool.wait_ge(zg_sem[q], n * (16 * TOPK))
                pool.wait_ge(zi_sem[q], n * 16)
                pool.tensor_tensor(zg[q], zg[q], zi[:, q:q + 1, :].to_broadcast([P, 2 * TOPK, D]), ALU.subtract
                                   ).then_inc(diff_done, 1)

            pool.wait_ge(z_lo_ready, 1)
            for q in range(2):
                double(q, q)
            pool.wait_ge(z_lo_ready, NS)
            with pool.Fori(0, NB // 2 - 1) as g:
                for q in range(2):
                    pool.wait_ge(scores_done, g * (2 * NS) + NS * (q + 1))
                    double(g * 2 + (q + 2), q)
                    gather_pairs(g * 2 + q, q, range(TOPK))
                    difference(g * 2 + q, q, g + 1)
            for q in range(2):
                gather_pairs(NB - 2 + q, q, range(TOPK))
                difference(NB - 2 + q, q, NB // 2)

            def gather(i, r, t, k):
                if k == 0:
                    pool.wait_ge(gidx_ready, i * BS + r + 1)
                    plain(pool)
                pool.indirect_dma_start(G[:, t, k, :], None, q_dram,
                                        bass.IndirectOffsetOnAxis(ap=gidx[:, t, k:k + 1], axis=0)
                                        ).then_inc(g_sem[t], 16)

            def tile_and_block(i, r, t):
                second_share(i * NS + r + QC, (i + r + 1) % NS,
                             [lambda k=k: gather(i, r, t, k) for k in range(TOPK)])

            pool.wait_ge(row_free, NB + 2)
            share_of_tile(TILES_B)
            for h in range(2):
                second_of_weights(QC, 1, h)
            for j0, j1, t in ((1, HB + 1, HB), (HB + 1, NS, NS - 1), (0, 1, NS)):
                pool.wait_ge(q_ready, t)
                pool.dma_start(q_dram[j0 * SB:j1 * SB, :].rearrange("(b p) d -> p b d", p=P),
                               Y[:, j0 * BS:j1 * BS, :]).then_inc(q_stored, 16)
            second_share(QC + 1, 2)
            pool.wait_ge(q_stored, 16 * 3)
            for k in range(TOPK):
                gather(0, 0, 0, k)
            second_share(QC + 2, 3, [lambda k=k: gather(0, 1, 1, k) for k in range(TOPK)])
            for k in range(TOPK):
                gather(0, 2, 0, k)

            def load_x(i):
                pool.wait_ge(ln_step, i * LN_OPS)
                plain(pool)
                pool.dma_start(xin, x_rows[bass.ds(i, 1), :, :, :].rearrange("i p b d -> (i p) b d")
                               ).then_inc(x_loaded, 16)

            def root(i):
                pool.wait_ge(ln_step, i * LN_OPS + (LN_OPS - 1))
                pool.tensor_tensor(stat[:, 3, :], stat[:, 3, :], mhalf[:, 0:BS], ALU.pow).then_inc(rstd_ready, 1)

            def store(i):
                pool.wait_ge(ln_step, (i + 1) * LN_OPS)
                plain(pool)
                pool.dma_start(out_rows[bass.ds(i, 1), :, :, :].rearrange("i p b d -> (i p) b d"),
                               osq).then_inc(out_stored, 16)

            load_x(0)
            tile_and_block(0, 3, 1)
            with pool.Fori(2, HB) as rr:
                for t in range(2):
                    tile_and_block(0, rr * 2 + t, t)
            with pool.Fori(1, NS) as i:
                for r in range(BS):
                    tile_and_block(i, r, r % 2)
                    if r == 4:
                        root(i - 1)
                store(i - 1)
                load_x(i)
            root(NS - 1)
            store(NS - 1)
            pool.wait_ge(out_stored, 16 * NS)



def kernel(x, adj, L0_gnn_W1, L0_gnn_b1, L0_gnn_W2, L0_gnn_b2):
    import numpy as np
    import concourse.bacc as bacc
    from concourse.bass_utils import run_bass_kernel_spmd

    a = np.asarray(adj).reshape(NS, SB, NS, BS, P).transpose(0, 2, 4, 3, 1)
    tiles = np.empty((NS * NS, P, BS, SB), a.dtype)
    for i in range(NS):
        for r in range(NS):
            tiles[i * NS + r] = a[i, (i + 1 + r) % NS]
    x = np.ascontiguousarray(x)
    arrays = {
        "at": tiles,
        "xt": np.ascontiguousarray(x.T),
        "x": x,
        "w12": np.concatenate([np.asarray(L0_gnn_W1), np.asarray(L0_gnn_W2)], axis=1),
        "b1": np.ascontiguousarray(L0_gnn_b1).reshape(D, 1),
        "b2": np.ascontiguousarray(L0_gnn_b2).reshape(1, D),
    }
    nc = bacc.Bacc("TRN2", target_bir_lowering=False, num_devices=1)
    ins = [nc.dram_tensor(name, a.shape, F32, kind="ExternalInput").ap() for name, a in arrays.items()]
    out = nc.dram_tensor("out", [N, D], F32, kind="ExternalOutput").ap()
    q_dram = nc.dram_tensor("q_dram", [N, D], F32).ap()
    z_dram = nc.dram_tensor("z_dram", [N // 2, 2 * D], F32).ap()
    xw2_dram = nc.dram_tensor("xw2_dram", [NB // HB, P, HB * D], F32).ap()
    gnn_kernel(nc, *ins, out, q_dram, xw2_dram, z_dram)
    r = run_bass_kernel_spmd(nc, [arrays], core_ids=[0])
    return r.results[0]["out"]
```
